# Optimizing a Trainium2 kernel written in Bass

```python
import numpy as np
import jax
import jax.numpy as jnp

def _softmax(x, axis=-1):
    return jax.nn.softmax(x, axis=axis)

def _gelu(x):
    return jax.nn.gelu(x, approximate=True)

def _silu(x):
    return jax.nn.silu(x)

def _sigmoid(x):
    return jax.nn.sigmoid(x)

def _layernorm(x, axis=-1, eps=1e-05):
    m = jnp.mean(x, axis=axis, keepdims=True)
    v = jnp.var(x, axis=axis, keepdims=True)
    return (x - m) / jnp.sqrt(v + eps)

def _scatter_add(tgt, idx, src, axis=0):
    return tgt.at[idx].add(src)

def _segment_sum(src, seg, n):
    return jax.ops.segment_sum(src, seg, n)
kernel_name = 'mk_cond_resid_d2_seqx_r8_51c48e'

def setup_inputs(seed: int=0):
    np.random.seed(seed)
    _w = jnp.asarray

    def _rec_inputs():
        import jax
        import jax.numpy as jnp
        _rk = jax.random.key(seed)
        x = -0.0003929 + 0.9999 * jax.random.normal(jax.random.fold_in(_rk, 1), (128, 32, 512), jnp.float32)
        _lenS = 32 - jax.random.randint(jax.random.fold_in(_rk, 7), (128,), 0, max(1, 32 // 4) + 1, jnp.int32)
        _lenS2 = 32 - jax.random.randint(jax.random.fold_in(_rk, 8), (128,), 0, max(1, 32 // 4) + 1, jnp.int32)
        itok_B_78_3631 = jax.random.randint(jax.random.fold_in(_rk, 11), (128,), 78, 454, jnp.int32)
        itok_B_6_15 = jax.random.randint(jax.random.fold_in(_rk, 12), (128,), 6, 16, jnp.int32)
        return (x, itok_B_78_3631, itok_B_6_15)
    x, itok_B_78_3631, itok_B_6_15 = _rec_inputs()

    def _L0_cond_setup():
        import math
        import jax, jax.numpy as jnp
        import numpy as np
        B, H, N, L = (16, 32, 64, 512)
        DT_MIN, DT_MAX = (0.001, 0.1)

        def _get_kernel(log_dt, C, log_A_real, A_imag, length):
            dt = jnp.exp(log_dt)
            Cc = C[..., 0] + 1j * C[..., 1]
            A = -jnp.exp(log_A_real) + 1j * A_imag
            dtA = A * dt[:, None]
            Ct = Cc * (jnp.exp(dtA) - 1.0) / A
            P = dtA[:, :, None] * jnp.arange(length, dtype=jnp.float32)
            K = 2.0 * jnp.einsum('hn,hnl->hl', Ct, jnp.exp(P)).real
            return K
        key = jax.random.key(seed)
        ks = jax.random.split(key, 5)
        u = jax.random.normal(ks[0], (B, H, L), dtype=jnp.float32)
        log_dt = jax.random.uniform(ks[1], (H,), dtype=jnp.float32) * (math.log(DT_MAX) - math.log(DT_MIN)) + math.log(DT_MIN)
        C = jax.random.normal(ks[2], (H, N, 2), dtype=jnp.float32)
        log_A_real = jnp.log(0.5 * jnp.ones((H, N), dtype=jnp.float32))
        A_imag = math.pi * jnp.broadcast_to(jnp.arange(N, dtype=jnp.float32), (H, N))
        D = jax.random.normal(ks[3], (H,), dtype=jnp.float32)
        length = jax.random.randint(ks[4], (B,), 1, L + 1, dtype=jnp.int32)
        return {'u': u, 'log_dt': log_dt, 'C': C, 'log_A_real': log_A_real, 'A_imag': A_imag, 'D': D, 'length': length}
    _L0_cond_all = _L0_cond_setup()
    _L0_cond_in = {k: v for k, v in _L0_cond_all.items() if k in ('log_dt', 'C', 'log_A_real', 'A_imag', 'D')}
    del _L0_cond_all

    def _L1_cond_setup():
        import jax, jax.numpy as jnp
        import numpy as np
        B, S, D_IN, D_OUT = (4, 256, 512, 512)
        RANK, MAX_LORAS = (16, 32)
        key = jax.random.key(seed)
        ks = jax.random.split(key, 6)
        x = jax.random.normal(ks[0], (B, S, D_IN), dtype=jnp.float32)
        adapter_ids = jax.random.randint(ks[1], (B,), 0, MAX_LORAS)
        base_weight = jax.random.normal(ks[2], (D_OUT, D_IN), dtype=jnp.float32) * D_IN ** (-0.5)
        base_bias = jax.random.normal(ks[3], (D_OUT,), dtype=jnp.float32) * 0.01
        lora_A_w = jax.random.normal(ks[4], (MAX_LORAS, RANK, D_IN), dtype=jnp.float32) * D_IN ** (-0.5)
        lora_B_w = jax.random.normal(ks[5], (MAX_LORAS, D_OUT, RANK), dtype=jnp.float32) * RANK ** (-0.5)
        return {'x': x, 'adapter_ids': adapter_ids, 'base_weight': base_weight, 'base_bias': base_bias, 'lora_A_w': lora_A_w, 'lora_B_w': lora_B_w}
    _L1_cond_all = _L1_cond_setup()
    _L1_cond_in = {k: v for k, v in _L1_cond_all.items() if k in ('base_weight', 'base_bias', 'lora_A_w', 'lora_B_w')}
    del _L1_cond_all
    return {'x': x, 'itok_B_78_3631': itok_B_78_3631, 'itok_B_6_15': itok_B_6_15, 'L0_cond_log_dt': _L0_cond_in['log_dt'], 'L0_cond_C': _L0_cond_in['C'], 'L0_cond_log_A_real': _L0_cond_in['log_A_real'], 'L0_cond_A_imag': _L0_cond_in['A_imag'], 'L0_cond_D': _L0_cond_in['D'], 'L1_cond_base_weight': _L1_cond_in['base_weight'], 'L1_cond_base_bias': _L1_cond_in['base_bias'], 'L1_cond_lora_A_w': _L1_cond_in['lora_A_w'], 'L1_cond_lora_B_w': _L1_cond_in['lora_B_w']}

def reference(x, itok_B_78_3631, itok_B_6_15, L0_cond_log_dt, L0_cond_C, L0_cond_log_A_real, L0_cond_A_imag, L0_cond_D, L1_cond_base_weight, L1_cond_base_bias, L1_cond_lora_A_w, L1_cond_lora_B_w):
    import jax
    import jax.numpy as jnp

    def _L0_cond_ref(u, log_dt, C, log_A_real, A_imag, D, length):
        import math
        import jax, jax.numpy as jnp
        import numpy as np
        B, H, N, L = (16, 32, 64, 512)
        DT_MIN, DT_MAX = (0.001, 0.1)

        def _get_kernel(log_dt, C, log_A_real, A_imag, length):
            dt = jnp.exp(log_dt)
            Cc = C[..., 0] + 1j * C[..., 1]
            A = -jnp.exp(log_A_real) + 1j * A_imag
            dtA = A * dt[:, None]
            Ct = Cc * (jnp.exp(dtA) - 1.0) / A
            P = dtA[:, :, None] * jnp.arange(length, dtype=jnp.float32)
            K = 2.0 * jnp.einsum('hn,hnl->hl', Ct, jnp.exp(P)).real
            return K
        Bq, Hq, Lq = u.shape
        K = _get_kernel(log_dt, C, log_A_real, A_imag, Lq)
        n = 2 * Lq
        kf = jnp.fft.rfft(K, n=n)
        uf = jnp.fft.rfft(u, n=n)
        y = jnp.fft.irfft(uf * kf[None], n=n)[..., :Lq]
        y = y + u * D[:, None]
        mask = (jnp.arange(Lq)[None, :] < length[:, None]).astype(u.dtype)
        return y * mask[:, None, :]

    def _L1_cond_ref(x, adapter_ids, base_weight, base_bias, lora_A_w, lora_B_w):
        import jax, jax.numpy as jnp
        import numpy as np
        B, S, D_IN, D_OUT = (4, 256, 512, 512)
        RANK, MAX_LORAS = (16, 32)
        result = jnp.einsum('bsd,od->bso', x, base_weight) + base_bias
        A = lora_A_w[adapter_ids]
        Bw = lora_B_w[adapter_ids]
        h = jnp.einsum('bsd,brd->bsr', x, A)
        lora_out = jnp.einsum('bsr,bor->bso', h, Bw)
        result = result + lora_out
        return result.astype(x.dtype)
    x = x + _L0_cond_ref(x, L0_cond_log_dt, L0_cond_C, L0_cond_log_A_real, L0_cond_A_imag, L0_cond_D, itok_B_78_3631)
    x = x + _L1_cond_ref(x, itok_B_6_15, L1_cond_base_weight, L1_cond_base_bias, L1_cond_lora_A_w, L1_cond_lora_B_w)
    return x

_drawn_inputs = setup_inputs


def setup_inputs(seed=0):
    import zlib

    import numpy as np

    out = dict(_drawn_inputs(seed))
    spreads = {'L0_cond_log_A_real': (-0.6931471824645996, 0.2)}
    factors = {'L1_cond_base_bias': 8.0}
    for name, (base, spread) in spreads.items():
        noise = np.random.default_rng([zlib.crc32(name.encode()), seed]).standard_normal(out[name].shape)
        drawn = base * np.exp(spread * noise) if base else spread * noise
        out[name] = jnp.asarray(drawn.astype(out[name].dtype))
    for name, factor in factors.items():
        out[name] = (out[name] * factor).astype(out[name].dtype)
    return out
```

```python
import math
from contextlib import ExitStack

import concourse.bass as bass
from concourse import mybir

F32 = mybir.dt.float32
F32R = mybir.dt.float32r
I32 = mybir.dt.int32
ALU = mybir.AluOpType
ACT = mybir.ActivationFunctionType

P = 128
NB, NH, L = 128, 32, 512
NS = 64
LC = L // P
AD, R = 32, 16
NA, NC = 16, 32
BT = P // NH
NT = NB // BT
BR = BT * R
PAD = P + L
assert NA * NC == L and 2 * NS == P

TWO_PI_HI = 6.28125
TWO_PI_LO = 2 * math.pi - TWO_PI_HI
ROUND = 1.5 * 2.0 ** 23

XS = 4
ZS = 2
TS = 2
BS = 4
OS = 4


def build(nc, x_conv, x_tile, params, phases, d_row, length, ids_row, w_t, bias, a_t, b_rows, out):
    ctx = ExitStack()
    with ctx:
        def sb(name, shape, dt=F32):
            return ctx.enter_context(nc.sbuf_tensor(name, shape, dt))

        def pb(name, shape):
            return ctx.enter_context(nc.psum_tensor(name, shape, F32))

        def sem(name):
            return ctx.enter_context(nc.semaphore(name))

        k_pad = nc.dram_tensor("k_pad", (NH, PAD), F32, kind="Internal").ap()

        par = sb("par", [P, 5, NH])
        ph = sb("ph", [P, 3, 4])
        dt = sb("dt", [P, NH])
        ea = sb("ea", [P, NH])
        zr = sb("zr", [P, NH])
        zi = sb("zi", [P, NH])
        sm = sb("sm", [P, 16, NH])
        li = sb("li", [P, NA + NC], I32)
        lf = sb("lf", [P, NA + NC])
        TA, TC = NH * NA, NH * NC
        gg = sb("gg", [P, NH, NA])
        g2 = sb("g2", [P, NH, NA])
        ee = sb("ee", [P, NH, NC])
        k_sb = sb("k_sb", [NA, NH, NC])
        d_at = sb("d_at", [NA, NH])
        zero = sb("zero", [NH, P])
        pos = sb("pos", [P, LC, NB], I32)
        len_sb = sb("len_sb", [P, NB], I32)
        mask = sb("mask", [P, LC, NB])
        x_in = sb("x_in", [P, XS, L])
        strip = sb("strip", [P, XS, L])
        z_all = sb("z_all", [P, LC, NB, NH])
        scratch = z_all[:, :, :, :].rearrange("p c b h -> p (c b h)")
        mag = scratch[:, 0:TA + TC].rearrange("p (h a) -> p h a", h=NH)
        ang = scratch[:, TA + TC:2 * (TA + TC)]
        o = 2 * (TA + TC)
        red = scratch[:, o:o + 2 * TA + TC]
        o += 2 * TA + TC
        trn = scratch[:, o:o + 2 * TA + TC]
        w_sb = sb("w_sb", [P, LC, L])
        w_hi = sb("w_hi", [P, LC, L], F32R)
        w_lo = sb("w_lo", [P, LC, L], F32R)
        eye = sb("eye", [P, P])
        a_raw = sb("a_raw", [P, AD, LC * R])
        a_hl = sb("a_hl", [P, AD, 2, LC * R], F32R)
        ids = sb("ids", [1, NB], I32)
        id_f = sb("id_f", [1, 2, NB])
        ag = sb("ag", [P, TS, 2, LC, 2, BT, R], F32R)
        own = sb("own", [P, BT, NH])
        bias_sb = sb("bias_sb", [P, L])
        x_t = sb("x_t", [P, TS, L])
        x_hi = sb("x_hi", [P, TS, LC, P], F32R)
        x_lo = sb("x_lo", [P, TS, LC, P], F32R)
        b_raw = sb("b_raw", [BR, BS, L])
        b_hl = sb("b_hl", [P, TS, L], F32R)
        h_m = sb("h_m", [P, TS, P])
        h_hi = sb("h_hi", [P, TS, P], F32R)
        h_lo = sb("h_lo", [BR, TS, P], F32R)
        o_sb = sb("o_sb", [P, OS, L])

        k_ps = pb("k_ps", [P, 2, L])
        z_ps = pb("z_ps", [P, ZS, L])
        y_ps = pb("y_ps", [P, TS, L])
        h_ps = pb("h_ps", [P, TS, L])

        par_in, phase_in, d_in, len_in, ids_in = (sem(n) for n in ("par_in", "phase_in", "d_in", "len_in", "ids_in"))
        w_in, a_in, bias_in = sem("w_in"), sem("a_in"), sem("bias_in")
        x_landed = [sem(f"x_landed{s}") for s in range(XS)]
        strip_landed = [sem(f"strip_landed{s}") for s in range(XS)]
        xt_landed = [sem(f"xt_landed{s}") for s in range(TS)]
        b_landed = [sem(f"b_landed{s}") for s in range(BS)]
        stored = [sem(f"stored{s}") for s in range(OS)]
        k_stored, pad_stored = sem("k_stored"), sem("pad_stored")
        pool_step, dve_step, act_step = sem("pool_step"), sem("dve_step"), sem("act_step")
        counters, exps0, z_ready = sem("counters"), sem("exps0"), sem("z_ready")
        mags, exps1, reduced, sines = sem("mags"), sem("exps1"), sem("reduced"), sem("sines")
        turn_ready = sem("turn_ready")
        factors, k_done, k_ready, zeroed = sem("factors"), sem("k_done"), sem("k_ready"), sem("zeroed")
        mask_ready, conv_done, x1_done = sem("mask_ready"), sem("conv_done"), sem("x1_done")
        z_masked = sem("z_masked")
        w_eye, w_hi_done, w_split = sem("w_eye"), sem("w_hi_done"), sem("w_split")
        a_hi_done, a_split, ids_ready, own_ready = sem("a_hi_done"), sem("a_split"), sem("ids_ready"), sem("own_ready")
        gathered = sem("gathered")
        xhi_done, xlo_done, bhi_done, blo_done = sem("xhi_done"), sem("xlo_done"), sem("bhi_done"), sem("blo_done")
        h_done, hm_done, hhi_done, hlo_done = sem("h_done"), sem("hm_done"), sem("hhi_done"), sem("hlo_done")
        base_done, y_done, o_done = sem("base_done"), sem("y_done"), sem("o_done")

        block = ctx.enter_context(nc.Block())

        @block.sync
        def _(sp):
            sp.dma_start(par[:, :, :], params).then_inc(par_in, 16)
            sp.dma_start(ph[:, :, :], phases).then_inc(phase_in, 16)
            sp.dma_start(ids[:, :], ids_row).then_inc(ids_in, 16)
            sp.wait_ge(zeroed, 2)
            sp.dma_start(d_at[0:1, :], d_row).then_inc(d_in, 16)
            sp.dma_start(k_pad[:, 0:P], zero[:, :]).then_inc(pad_stored, 16)
            sp.dma_start(len_sb[:, :], length.to_broadcast((P, NB))).then_inc(len_in, 16)

            def load_x(h, s):
                sp.dma_start(x_in[:, s, :], x_conv[h]).then_inc(x_landed[s], 16)

            for s in range(XS):
                load_x(s, s)
            sp.dma_start(w_sb[:, :, :], w_t).then_inc(w_in, 16)
            sp.dma_start(a_raw[:, :, :], a_t).then_inc(a_in, 16)
            sp.dma_start(bias_sb[:, :], bias.to_broadcast((P, L))).then_inc(bias_in, 16)

            with sp.Fori(1, NH // XS) as lap:
                for s in range(XS):
                    sp.wait_ge(conv_done, lap * XS + (s + 1 - XS))
                    load_x(lap * XS + s, s)

            sp.wait_ge(ids_ready, 4)

            def load_b(t, s):
                for q in range(BT):
                    i = sp.value_load(ids[0:1, bass.ds(t * BT + q, 1)], min_val=0, max_val=AD - 1)
                    sp.dma_start(b_raw[R * q:R * (q + 1), s, :],
                                 b_rows[bass.ds(i * R, R), :]).then_inc(b_landed[s], 16)

            def load_x_tile(t, s):
                sp.dma_start(x_t[:, s, :], x_tile[t]).then_inc(xt_landed[s], 16)

            def store(t, s):
                sp.wait_ge(o_done, t + 1)
                sp.dma_start(out[bass.ds(t * P, P), :], o_sb[:, s, :]).then_inc(stored[s], 16)

            for t in range(TS):
                load_x_tile(t, t)
            for t in range(BS):
                load_b(t, t)
            for t in range(TS, BS):
                sp.wait_ge(xlo_done, t + (1 - TS))
                load_x_tile(t, t % TS)
            with sp.Fori(1, NT // BS) as lap:
                for s in range(BS):
                    t = lap * BS + s
                    sp.wait_ge(bhi_done, t + (1 - BS))
                    sp.wait_ge(blo_done, t + (1 - BS))
                    load_b(t, s)
                    sp.wait_ge(xlo_done, t + (1 - TS))
                    load_x_tile(t, s % TS)
                    store(t - BS, s)
            for s in range(OS):
                store(NT - OS + s, s)
            for s in range(OS):
                sp.wait_ge(stored[s], 16 * (NT // OS))

        @block.gpsimd
        def _(pool):
            steps = [0]

            def link(ins):
                steps[0] += 1
                ins.then_inc(pool_step, 1)
                pool.wait_ge(pool_step, steps[0])

            nc.gpsimd.iota(li[:, 0:NA], pattern=[[NC, NA]], base=0, channel_multiplier=0)
            nc.gpsimd.iota(li[:, NA:NA + NC], pattern=[[1, NC]], base=0,
                           channel_multiplier=0).then_inc(counters, 1)
            nc.gpsimd.memset(d_at[:, :], 0.0).then_inc(zeroed, 1)
            nc.gpsimd.memset(zero[:, :], 0.0).then_inc(zeroed, 1)
            pool.wait_ge(turn_ready, 1)
            pool.wait_ge(z_ready, 1)
            nc.gpsimd.tensor_tensor(mag[:, :, :], zr[:, :].unsqueeze(2).to_broadcast((P, NH, NA + NC)),
                                    lf[:, :].unsqueeze(1).to_broadcast((P, NH, NA + NC)),
                                    ALU.mult).then_inc(mags, 1)
            nc.gpsimd.iota(pos[:, :, :], pattern=[[P, LC], [0, NB]], base=0,
                           channel_multiplier=1).then_inc(counters, 1)
            link(nc.gpsimd.memset(eye[:, :], 0.0))
            link(nc.gpsimd.affine_select(out=eye[:, :], in_=eye[:, :], compare_op=ALU.not_equal, fill=1.0,
                                         base=0, pattern=[[-1, P]], channel_multiplier=1))
            link(nc.gpsimd.memset(own[:, :, :], 1.0))
            for o in (0, BR):
                half = own[o:o + BR, :, :]
                link(nc.gpsimd.affine_select(out=half, in_=half, compare_op=ALU.is_ge, fill=0.0, base=0,
                                             pattern=[[-R, BT], [0, NH]], channel_multiplier=1))
                nc.gpsimd.affine_select(out=half, in_=half, compare_op=ALU.is_ge, fill=0.0, base=R - 1,
                                        pattern=[[R, BT], [0, NH]], channel_multiplier=-1).then_inc(own_ready, 1)
                pool.wait_ge(own_ready, 1 + o // BR)
            pool.wait_ge(w_in, 16)
            for c in range(LC):
                d = w_sb[:, c, c * P:(c + 1) * P]
                nc.gpsimd.tensor_tensor(d, d, eye[:, :], ALU.add).then_inc(w_eye, 1)
            pool.wait_ge(a_hi_done, 1)
            nc.gpsimd.tensor_tensor(a_hl[:, :, 1, :], a_raw[:, :, :], a_hl[:, :, 0, :].bitcast(F32),
                                    ALU.subtract).then_inc(a_split, 1)
            pool.wait_ge(w_hi_done, 1)
            pool.wait_ge(w_eye, LC)
            nc.gpsimd.tensor_tensor(w_lo[:, :, :], w_sb[:, :, :], w_hi[:, :, :].bitcast(F32),
                                    ALU.subtract).then_inc(w_split, 1)
            pool.wait_ge(a_split, 1)
            pool.wait_ge(ids_ready, 4)

            def gather(t, s):
                for q in range(BT):
                    i = pool.value_load(ids[0:1, bass.ds(t * BT + q, 1)], min_val=0, max_val=AD - 1)
                    src = a_hl[:, bass.ds(i, 1), :, :].bitcast(F32).rearrange("p o e (c r) -> p (o e c) r", c=LC)
                    for d in range(2):
                        last = nc.gpsimd.tensor_copy(
                            ag[:, s, :, :, d, q, :].rearrange("p e c r -> p (e c) r"), src)
                last.then_inc(gathered, 1)

            for t in range(TS):
                gather(t, t)
            with pool.Fori(1, NT // TS) as lap:
                for s in range(TS):
                    pool.wait_ge(h_done, lap * TS + (s + 1 - TS))
                    gather(lap * TS + s, s)

        @block.scalar
        def _(act):
            act.wait_ge(par_in, 16)
            nc.scalar.activation(dt[:, :], par[:, 4, :], ACT.Exp).then_inc(exps0, 1)
            nc.scalar.activation(ea[:, :], par[:, 0, :], ACT.Exp).then_inc(exps0, 1)
            act.wait_ge(z_ready, 1)
            nc.scalar.activation(sm[:, 0, :], zr[:, :], ACT.Exp).then_inc(exps1, 1)
            act.wait_ge(mags, 1)
            nc.scalar.activation(mag[:, :, :], mag[:, :, :], ACT.Exp).then_inc(exps1, 1)
            act.wait_ge(phase_in, 16)
            act.wait_ge(reduced, 1)
            nc.scalar.activation(sm[:, 1:3, :], sm[:, 3:5, :], ACT.Sin).then_inc(sines, 1)
            for n, (o, e) in enumerate(((0, TA), (TA, 2 * TA), (2 * TA, 2 * TA + TC))):
                act.wait_ge(reduced, n + 2)
                nc.scalar.activation(trn[:, o:e], red[:, o:e], ACT.Sin, bias=ph[:, n, 0:1]).then_inc(sines, 1)

            def load_strip(h, s):
                row = k_pad[bass.ds(h, 1), 1:1 + L]
                src = bass.AP(tensor=row.tensor, offset=row.offset, ap=[[1, P], [1, L]])
                act.dma_start(strip[:, s, :], src).then_inc(strip_landed[s], 16)

            act.wait_ge(a_in, 16)
            nc.scalar.activation(a_hl[:, :, 0, :], a_raw[:, :, :], ACT.Copy).then_inc(a_hi_done, 1)
            act.wait_ge(w_eye, LC)
            nc.scalar.activation(w_hi[:, :, :], w_sb[:, :, :], ACT.Copy).then_inc(w_hi_done, 1)
            act.wait_ge(k_ready, 2)
            act.dma_start(k_pad[:, P:PAD].rearrange("h (a c) -> a h c", a=NA), k_sb[:, :, :]).then_inc(k_stored, 16)
            act.wait_ge(k_stored, 16)
            act.wait_ge(pad_stored, 16)
            for s in range(XS):
                load_strip(s, s)
            with act.Fori(1, NH // XS) as lap:
                for s in range(XS):
                    act.wait_ge(conv_done, lap * XS + (s + 1 - XS))
                    load_strip(lap * XS + s, s)

            def tile_in(t, s, first):
                act.wait_ge(x1_done, t + 1)
                if not first:
                    act.wait_ge(base_done, t + (1 - TS))
                act.activation(x_hi[:, s % TS, :, :].rearrange("p c n -> p (c n)"), x_t[:, s % TS, :],
                               ACT.Copy).then_inc(xhi_done, 1)

            def tile_b(t, s, lap, first):
                act.wait_ge(b_landed[s % BS], 16 * BT * (lap + 1))
                if not first:
                    act.wait_ge(y_done, t + (1 - TS))
                act.activation(b_hl[0:BR, s % TS, :], b_raw[:, s % BS, :], ACT.Copy).then_inc(bhi_done, 1)

            def tile_h(t, s, first):
                act.wait_ge(hm_done, t + 1)
                if not first:
                    act.wait_ge(y_done, t + (1 - TS))
                act.activation(h_hi[:, s % TS, :], h_m[:, s % TS, :], ACT.Copy).then_inc(hhi_done, 1)

            tile_in(0, 0, True)
            tile_b(0, 0, 0, True)
            for t in range(1, BS):
                tile_in(t, t, t < TS)
                tile_h(t - 1, t - 1, t - 1 < TS)
                tile_b(t, t, 0, t < TS)
            with act.Fori(1, NT // BS) as lap:
                for s in range(BS):
                    t = lap * BS + s
                    tile_in(t, s, False)
                    tile_h(t - 1, s + BS - 1, False)
                    tile_b(t, s, lap, False)
            tile_h(NT - 1, BS - 1, False)

        @block.vector
        def _(dve):
            steps = [0]

            def link(ins):
                steps[0] += 1
                ins.then_inc(dve_step, 1)
                dve.wait_ge(dve_step, steps[0])

            V = nc.vector
            dve.wait_ge(counters, 1)
            V.tensor_copy(lf[:, :], li[:, :]).then_inc(turn_ready, 1)
            dve.wait_ge(par_in, 16)
            dve.wait_ge(exps0, 2)
            V.scalar_tensor_tensor(zr[:, :], ea[:, :], -1.0, dt[:, :], ALU.mult, ALU.mult).then_inc(z_ready, 1)
            link(V.tensor_tensor(zi[:, :], par[:, 1, :], dt[:, :], ALU.mult))
            dve.wait_ge(turn_ready, 1)
            V.tensor_tensor(ang[:, 0:TA].rearrange("p (h a) -> p h a", a=NA),
                            zi[:, :].unsqueeze(2).to_broadcast((P, NH, NA)),
                            lf[:, 0:NA].unsqueeze(1).to_broadcast((P, NH, NA)), ALU.mult).then_inc(dve_step, 1)
            link(V.tensor_tensor(ang[:, TA:TA + TC].rearrange("p (h a) -> p h a", a=NC),
                                 zi[:, :].unsqueeze(2).to_broadcast((P, NH, NC)),
                                 lf[:, NA:NA + NC].unsqueeze(1).to_broadcast((P, NH, NC)), ALU.mult))
            steps[0] += 1
            dve.wait_ge(dve_step, steps[0])

            def reduce_angle(dst, tmp, src, phase, turns, lo, hi):
                link(V.tensor_scalar(tmp, src, 1 / (2 * math.pi), turns, ALU.mult, ALU.add))
                link(V.tensor_scalar(tmp, tmp, ROUND, -ROUND, ALU.add, ALU.add))
                link(V.scalar_tensor_tensor(dst, tmp, -TWO_PI_HI, src, ALU.mult, ALU.add))
                link(V.scalar_tensor_tensor(dst, tmp, -TWO_PI_LO, dst, ALU.mult, ALU.add))
                return V.tensor_scalar(dst, dst, lo, hi, ALU.max, ALU.min)

            PI = 3.1415925
            link(reduce_angle(sm[:, 3, :], sm[:, 5, :], zi[:, :], 0.0, 0.0, -PI, PI))
            link(reduce_angle(sm[:, 6, :], sm[:, 5, :], zi[:, :], 0.0, 0.25, -PI - math.pi / 2, PI - math.pi / 2))
            link(V.tensor_scalar(sm[:, 4, :], sm[:, 6, :], math.pi / 2, PI, ALU.add, ALU.min))
            V.tensor_scalar(sm[:, 4, :], sm[:, 4, :], -PI, None, ALU.max).then_inc(reduced, 1)
            dve.wait_ge(phase_in, 16)
            for n, (src, o) in enumerate(((ang[:, 0:TA], 0), (ang[:, 0:TA], TA), (ang[:, TA:TA + TC], 2 * TA))):
                w = src.shape[1]
                reduce_angle(red[:, o:o + w], trn[:, o:o + w], src, None, ph[:, n, 1:2],
                             ph[:, n, 2:3], ph[:, n, 3:4]).then_inc(reduced, 1)
            nr, ni, den, t1, t2, qr, qi = (sm[:, k, :] for k in (7, 8, 9, 10, 11, 12, 13))
            cr, ci = sm[:, 14, :], sm[:, 15, :]
            ai = par[:, 1, :]
            dve.wait_ge(exps1, 1)
            dve.wait_ge(sines, 1)
            link(V.tensor_tensor(nr, sm[:, 0, :], sm[:, 2, :], ALU.mult))
            link(V.tensor_scalar(nr, nr, -1.0, None, ALU.add))
            link(V.tensor_tensor(ni, sm[:, 0, :], sm[:, 1, :], ALU.mult))
            link(V.tensor_tensor(t1, ea[:, :], ea[:, :], ALU.mult))
            link(V.tensor_tensor(t2, ai, ai, ALU.mult))
            link(V.tensor_tensor(t1, t1, t2, ALU.add))
            link(V.reciprocal(den, t1))
            link(V.tensor_tensor(t1, nr, ea[:, :], ALU.mult))
            link(V.tensor_tensor(t2, ni, ai, ALU.mult))
            link(V.tensor_tensor(t2, t2, t1, ALU.subtract))
            link(V.scalar_tensor_tensor(qr, t2, 2.0, den, ALU.mult, ALU.mult))
            link(V.tensor_tensor(t1, ni, ea[:, :], ALU.mult))
            link(V.tensor_tensor(t2, nr, ai, ALU.mult))
            link(V.tensor_tensor(t2, t2, t1, ALU.add))
            link(V.scalar_tensor_tensor(qi, t2, -2.0, den, ALU.mult, ALU.mult))
            link(V.tensor_tensor(t1, par[:, 2, :], qr, ALU.mult))
            link(V.tensor_tensor(t2, par[:, 3, :], qi, ALU.mult))
            link(V.tensor_tensor(cr, t1, t2, ALU.subtract))
            link(V.tensor_tensor(t1, par[:, 2, :], qi, ALU.mult))
            link(V.tensor_tensor(t2, par[:, 3, :], qr, ALU.mult))
            link(V.tensor_tensor(ci, t1, t2, ALU.add))
            f1 = trn[:, 0:TA].rearrange("p (h a) -> p h a", a=NA)
            f2 = trn[:, TA:2 * TA].rearrange("p (h a) -> p h a", a=NA)
            fe = trn[:, 2 * TA:2 * TA + TC].rearrange("p (h a) -> p h a", a=NC)
            dve.wait_ge(exps1, 2)
            dve.wait_ge(sines, 3)
            link(V.tensor_tensor(gg[:, :, :], f1, cr.unsqueeze(2).to_broadcast((P, NH, NA)), ALU.mult))
            link(V.tensor_tensor(g2[:, :, :], f2, ci.unsqueeze(2).to_broadcast((P, NH, NA)), ALU.mult))
            link(V.tensor_tensor(gg[:, :, :], gg[:, :, :], g2[:, :, :], ALU.add))
            V.tensor_tensor(gg[:, :, :], gg[:, :, :], mag[:, :, 0:NA], ALU.mult).then_inc(factors, 1)
            dve.wait_ge(sines, 4)
            V.tensor_tensor(ee[:, :, :], fe, mag[:, :, NA:NA + NC], ALU.mult).then_inc(factors, 1)
            dve.wait_ge(k_done, 1)
            link(V.tensor_copy(k_sb[:, :, :], k_ps[0:NA, :, :].rearrange("p u (h c) -> p (u h) c", c=NC)))
            k_0 = k_sb[:, :, 0]
            dve.wait_ge(d_in, 16)
            V.tensor_tensor(k_0, k_0, d_at[:, :], ALU.add).then_inc(k_ready, 2)
            dve.wait_ge(ids_in, 16)
            V.tensor_scalar(id_f[:, 0, :], ids[:, :], 0.0, float(AD), ALU.is_lt, ALU.mult).then_inc(ids_ready, 1)
            dve.wait_ge(ids_ready, 1)
            V.tensor_tensor(id_f[:, 1, :], ids[:, :], id_f[:, 0, :], ALU.add).then_inc(ids_ready, 1)
            dve.wait_ge(ids_ready, 2)
            V.tensor_scalar(id_f[:, 0, :], id_f[:, 1, :], 0.0, float(AD - 1), ALU.max, ALU.min).then_inc(ids_ready, 1)
            dve.wait_ge(ids_ready, 3)
            V.tensor_copy(ids[:, :], id_f[:, 0, :]).then_inc(ids_ready, 1)
            dve.wait_ge(counters, 2)
            dve.wait_ge(len_in, 16)
            link(V.tensor_tensor(mask[:, :, :], pos[:, :, :],
                                 len_sb[:, :].unsqueeze(1).to_broadcast((P, LC, NB)), ALU.is_lt))

            m2 = mask[:, :, :].rearrange("p c b -> p (c b)")

            def head(h, s):
                dve.wait_ge(conv_done, h + 1)
                V.tensor_tensor(z_all[:, :, :, bass.ds(h, 1)].rearrange("p c b o -> p (c b o)"),
                                z_ps[:, s % ZS, :], m2, ALU.mult).then_inc(z_masked, 1)

            with dve.Fori(0, NH // ZS) as lap:
                for s in range(ZS):
                    head(lap * ZS + s, s)

            def tile_x1(t, s, lap):
                dve.wait_ge(xt_landed[s % TS], 16 * (lap + 1))
                xt = x_t[:, s % TS, :].rearrange("p (c n) -> p c n", c=LC)
                V.tensor_tensor(xt, xt, z_all[:, :, bass.ds(t * BT, BT), :].rearrange("p c b h -> p c (b h)"),
                                ALU.add).then_inc(x1_done, 1)

            def tile_in(t, s, first):
                dve.wait_ge(xhi_done, t + 1)
                if not first:
                    dve.wait_ge(base_done, t + (1 - TS))
                V.tensor_tensor(x_lo[:, s % TS, :, :].rearrange("p c n -> p (c n)"), x_t[:, s % TS, :],
                                x_hi[:, s % TS, :, :].rearrange("p c n -> p (c n)").bitcast(F32),
                                ALU.subtract).then_inc(xlo_done, 1)

            def tile_b(t, s, first):
                dve.wait_ge(bhi_done, t + 1)
                if not first:
                    dve.wait_ge(y_done, t + (1 - TS))
                V.tensor_tensor(b_hl[BR:P, s % TS, :], b_raw[:, s % BS, :],
                                b_hl[0:BR, s % TS, :].bitcast(F32), ALU.subtract).then_inc(blo_done, 1)

            def tile_h(t, s, first):
                dve.wait_ge(h_done, t + 1)
                V.tensor_tensor(h_m[:, s % TS, :], h_ps[:, s % TS, 0:P],
                                own[:, :, :].rearrange("p b h -> p (b h)"), ALU.mult).then_inc(hm_done, 1)
                dve.wait_ge(hhi_done, t + 1)
                if not first:
                    dve.wait_ge(y_done, t + (1 - TS))
                V.tensor_tensor(h_lo[:, s % TS, :], h_m[0:BR, s % TS, :],
                                h_hi[0:BR, s % TS, :].bitcast(F32), ALU.subtract).then_inc(hlo_done, 1)

            def tile_out(t, s, lap, first):
                dve.wait_ge(y_done, t + 1)
                if not first:
                    dve.wait_ge(stored[s % OS], 16 * lap)
                V.tensor_tensor(o_sb[:, s % OS, :], y_ps[:, s % TS, :], bias_sb[:, :],
                                ALU.add).then_inc(o_done, 1)

            dve.wait_ge(own_ready, 2)
            dve.wait_ge(bias_in, 16)
            dve.wait_ge(z_masked, NH)

            def step(t, s, lap, free, out_free):
                last = isinstance(t, int) and t >= NT
                if not isinstance(t, int) or t >= 2:
                    tile_out(t - 2, s - 2, lap if s >= 2 else lap - 1, out_free)
                if not last:
                    tile_x1(t, s, lap * (OS // TS) + s // TS)
                    tile_in(t, s, free)
                if not isinstance(t, int) or 1 <= t <= NT:
                    tile_h(t - 1, s - 1, isinstance(t, int) and t - 1 < TS)
                if not last:
                    tile_b(t, s, free)

            for s in range(OS):
                step(s, s, 0, s < TS, True)
            for s in range(2):
                step(OS + s, s, 1, False, True)
            for s in range(2, OS):
                step(OS + s, s, 1, False, False)
            with dve.Fori(2, NT // OS) as lap:
                for s in range(OS):
                    step(lap * OS + s, s, lap, False, False)
            for s in range(2):
                step(NT + s, s, NT // OS, False, False)

        @block.tensor
        def _(pe):
            pe.wait_ge(factors, 2)
            for h in range(NH):
                u, o = divmod(h * NC, L)
                last = nc.tensor.matmul(k_ps[0:NA, u, o:o + NC], gg[:, h, :], ee[:, h, :], start=True, stop=True)
            last.then_inc(k_done, 1)

            def head(s, lap, evacuated):
                pe.wait_ge(x_landed[s], 16 * (lap + 1))
                pe.wait_ge(strip_landed[s], 16 * (lap + 1))
                if evacuated is not None:
                    pe.wait_ge(z_masked, evacuated)
                for m in range(LC):
                    last = nc.tensor.matmul(z_ps[:, s % ZS, m * P:L], strip[:, s, m * P:(m + 1) * P], x_in[:, s, 0:L - m * P],
                                            start=(m == 0), stop=(m == LC - 1))
                last.then_inc(conv_done, 1)

            for s in range(XS):
                head(s, 0, s + 1 - ZS if s >= ZS else None)
            with pe.Fori(1, NH // XS) as lap:
                for s in range(XS):
                    head(s, lap, lap * XS + (s + 1 - ZS))

            def tile(t, s, first):
                s %= TS
                pe.wait_ge(gathered, t + 1)
                pe.wait_ge(xhi_done, t + 1)
                pe.wait_ge(xlo_done, t + 1)
                if not first:
                    pe.wait_ge(hm_done, t + (1 - TS))
                terms = [(c, a, x) for c in range(LC) for a, x in ((0, x_hi), (0, x_lo), (1, x_hi))]
                for n, (c, a, x) in enumerate(terms):
                    last = nc.tensor.matmul(h_ps[:, s, 0:P], ag[:, s, a, c, :, :, :].rearrange("p d b r -> p (d b r)"),
                                            x[:, s, c, :], start=(n == 0), stop=(n == len(terms) - 1))
                last.then_inc(h_done, 1)
                if not first:
                    pe.wait_ge(o_done, t + (1 - TS))
                terms = [(c, x, w) for c in range(LC) for x, w in ((x_hi, w_hi), (x_hi, w_lo), (x_lo, w_hi))]
                for n, (c, x, w) in enumerate(terms):
                    last = nc.tensor.matmul(y_ps[:, s, :], x[:, s, c, :], w[:, c, :], start=(n == 0), stop=False)
                last.then_inc(base_done, 1)
                pe.wait_ge(bhi_done, t + 1)
                pe.wait_ge(blo_done, t + 1)
                pe.wait_ge(hhi_done, t + 1)
                pe.wait_ge(hlo_done, t + 1)
                nc.tensor.matmul(y_ps[:, s, :], h_hi[:, s, :], b_hl[:, s, :], start=False, stop=False)
                nc.tensor.matmul(y_ps[:, s, :], h_lo[:, s, :], b_hl[0:BR, s, :],
                                 start=False, stop=True).then_inc(y_done, 1)

            pe.wait_ge(w_hi_done, 1)
            pe.wait_ge(w_split, 1)
            for t in range(TS):
                tile(t, t, True)
            with pe.Fori(1, NT // TS) as lap:
                for s in range(TS):
                    tile(lap * TS + s, s, False)


def kernel(**inputs):
    import numpy as np
    import concourse.bacc as bacc
    from concourse.bass_utils import run_bass_kernel_spmd

    g = {k: np.asarray(v) for k, v in inputs.items()}

    def both(a):
        return np.concatenate([a.T, a.T], axis=0)

    c = g["L0_cond_C"]
    params = np.stack([both(g["L0_cond_log_A_real"]), both(g["L0_cond_A_imag"]), both(c[..., 0]), both(c[..., 1]),
                       np.broadcast_to(g["L0_cond_log_dt"][None, :], (P, NH))], axis=1)
    pi, top = math.pi, 3.1415925
    phases = np.zeros((P, 3, 4), np.float32)
    for half, angles in enumerate(((pi / 2, pi, pi / 2), (0.0, pi / 2, pi))):
        for n, a in enumerate(angles):
            phases[half * NS:(half + 1) * NS, n] = (a, a / (2 * pi), -top - a, top - a)
    arrays = {
        "x_conv": g["x"].transpose(1, 2, 0).reshape(NH, LC, P, NB).transpose(0, 2, 1, 3)[:, ::-1].reshape(NH, P, L),
        "x_tile": g["x"].reshape(NT, P, LC, P).transpose(0, 3, 2, 1).reshape(NT, P, L),
        "params": params,
        "phases": phases,
        "d_row": g["L0_cond_D"].reshape(1, NH),
        "length": g["itok_B_78_3631"].reshape(1, NB),
        "ids_row": g["itok_B_6_15"].reshape(1, NB),
        "w_t": g["L1_cond_base_weight"].T.reshape(LC, P, L).transpose(1, 0, 2),
        "bias": g["L1_cond_base_bias"].reshape(1, L),
        "a_t": g["L1_cond_lora_A_w"].reshape(AD, R, LC, P).transpose(3, 0, 2, 1).reshape(P, AD, LC * R),
        "b_rows": g["L1_cond_lora_B_w"].transpose(0, 2, 1).reshape(AD * R, L),
    }
    arrays = {k: np.ascontiguousarray(v) for k, v in arrays.items()}
    nc = bacc.Bacc("TRN2", target_bir_lowering=False, num_devices=1)
    args = [nc.dram_tensor(k, a.shape, mybir.dt.from_np(a.dtype), kind="ExternalInput").ap()
            for k, a in arrays.items()]
    args.append(nc.dram_tensor("out", (NB * NH, L), F32, kind="ExternalOutput").ap())
    build(nc, *args)
    r = run_bass_kernel_spmd(nc, [arrays], core_ids=[0])
    return r.results[0]["out"].reshape(NB, NH, L)
```

```python
import math
from contextlib import ExitStack

import concourse.bass as bass
from concourse import mybir

F32 = mybir.dt.float32
F32R = mybir.dt.float32r
I32 = mybir.dt.int32
ALU = mybir.AluOpType
ACT = mybir.ActivationFunctionType

P = 128
NB, NH, L = 128, 32, 512
NS = 64
LC = L // P
AD, R = 32, 16
NA, NC = 16, 32
BT = P // NH
NT = NB // BT
BR = BT * R
PAD = P + L
assert NA * NC == L and 2 * NS == P

TWO_PI_HI = 6.28125
TWO_PI_LO = 2 * math.pi - TWO_PI_HI
PI = 3.1415925
ROUND = 1.5 * 2.0 ** 23

G = 8
NG = NH // G
NF = 2 * NA + NC
LOG2_E = 1 / math.log(2)
LN2_HI = 0.693359375
LN2_LO = math.log(2) - LN2_HI

XS = 4
CS = 4
ZS = 4
KS = 2
TS = 2
HS = CS
BS = XS
OS = XS
NW = 4
NU = 20
QA = 2
BC = AD * R // NW
assert G * NF == TS * 2 * P
assert BC == P and NW == LC and 2 * BR == P


def build(nc, x_conv, x_tile, params, table, d_row, length, ids_all, w_t, bias, a_t, b_rows, row_of, out):
    ctx = ExitStack()
    with ctx:
        def sb(name, shape, dt=F32):
            return ctx.enter_context(nc.sbuf_tensor(name, shape, dt))

        def pb(name, shape):
            return ctx.enter_context(nc.psum_tensor(name, shape, F32))

        def sem(name):
            return ctx.enter_context(nc.semaphore(name))

        k_pad = nc.dram_tensor("k_pad", (NH, PAD), F32, kind="Internal").ap()
        b_tab = nc.dram_tensor("b_tab", (2 * AD * R, L), F32, kind="Internal").ap()

        par = sb("par", [P, 7, NH])
        tab = sb("tab", [P, 3, NF])
        dt = sb("dt", [P, NH])
        ea = sb("ea", [P, NH])
        zr = sb("zr", [P, NH])
        zi = sb("zi", [P, NH])
        ez = sb("ez", [P, NH])
        ex = sb("ex", [P, 4, NH])
        ex_i = sb("ex_i", [P, NH], I32)
        ez_i = sb("ez_i", [P, NH], I32)
        an = sb("an", [P, 2, 2, NH])
        cs = sb("cs", [P, 2, NH])
        cs_m = sb("cs_m", [P, 4, NH])
        sm = sb("sm", [P, 16, NH])
        mag = sb("mag", [P, NH, NA + NC])
        ang = sb("ang", [P, G, NF])
        trn = sb("trn", [P, G, NF])
        red = sb("red", [P, G, NF])
        sines = sb("sines", [P, G, NF])
        gg = sb("gg", [P, KS, G, NA])
        g2 = sb("g2", [P, G, NA])
        ee = sb("ee", [P, KS, G, NC])
        k_sb = sb("k_sb", [NA, KS, G * NC])
        d_sb = sb("d_sb", [1, NH * NC])
        row0 = sb("row0", [1, NA])
        zero = sb("zero", [NH, P])
        len_sb = sb("len_sb", [P, NB], I32)
        mask = sb("mask", [P, LC, NB])
        pos = mask[:, :, :].bitcast(I32)
        x_in = sb("x_in", [P, XS, L])
        strip = sb("strip", [P, XS, L], F32R)
        xp = sb("xp", [P, CS, LC, 2, P], F32R)
        s_hi = sb("s_hi", [P, CS, L], F32R)
        z_all = sb("z_all", [P, LC, NB, NH])
        w_sb = sb("w_sb", [P, LC, L])
        w_hi = sb("w_hi", [P, LC, L], F32R)
        w_lo = sb("w_lo", [P, LC, L], F32R)
        eye = sb("eye", [P, P])
        a_raw = sb("a_raw", [P, AD, LC * R])
        a_hl = sb("a_hl", [P, AD, 2, LC * R], F32R)
        ids = sb("ids", [P, NB + NT], I32)
        id_f = sb("id_f", [P, 2, NB + NT])
        row_c = sb("row_c", [P, 1])
        b_now = sb("b_now", [P, XS], I32)
        b_idx = sb("b_idx", [P, NT], I32)
        ag = sb("ag", [P, TS, LC, 2, BT, R], F32R)
        own = sb("own", [BR, BT, NH])
        bias_sb = sb("bias_sb", [P, L])
        x_t = sb("x_t", [P, TS, L])
        bt_hl = sb("bt_hl", [P, 2, L], F32R)
        b_hl = strip
        o_sb = x_in
        h_b = ang[0:BR, :, :].rearrange("p g f -> p (g f)").rearrange("p (t m) -> p t m", t=TS)
        h_s = trn[0:BR, :, :].rearrange("p g f -> p (g f)").rearrange("p (t m) -> p t m", t=TS)
        h_m = sb("h_m", [BR, TS, P])
        h_hi = sb("h_hi", [P, TS, P], F32R)
        h_lo = sb("h_lo", [BR, TS, P], F32R)

        k_ps = pb("k_ps", [P, KS, L])
        z_ps = pb("z_ps", [P, ZS, L])
        y_ps = pb("y_ps", [P, TS, L])
        h_ps = z_ps

        par_in, table_in, d_in, len_in, ids_in = (sem(n) for n in ("par_in", "table_in", "d_in", "len_in", "ids_in"))
        w_in, a_in, bias_in = sem("w_in"), sem("a_in"), sem("bias_in")
        x_landed = [sem(f"x_landed{s}") for s in range(XS)]
        strip_landed = [sem(f"strip_landed{s}") for s in range(XS)]
        xt_landed = [sem(f"xt_landed{s}") for s in range(TS)]
        chunk_in = [sem(f"chunk_in{s}") for s in range(TS)]
        row_in, tab_hi_stored, tab_lo_stored = sem("row_in"), sem("tab_hi_stored"), sem("tab_lo_stored")
        b_landed = [sem(f"b_landed{s}") for s in range(BS)]
        stored = [sem(f"stored{s}") for s in range(OS)]
        k_stored, pad_stored = sem("k_stored"), sem("pad_stored")
        pool_step, dve_step = sem("pool_step"), sem("dve_step")
        pos_ready, zeroed, ea_ready, zr_ready, ez_ready = (
            sem(n) for n in ("pos_ready", "zeroed", "ea_ready", "zr_ready", "ez_ready"))
        den_ready, exponents, mags, angle_ready, cs_ready, ct_ready = (
            sem(n) for n in ("den_ready", "exponents", "mags", "angle_ready", "cs_ready", "ct_ready"))
        reduced, sines_ready, factors, k_done, k_copied = (
            sem(n) for n in ("reduced", "sines_ready", "factors", "k_done", "k_copied"))
        conv_done, z_masked = sem("conv_done"), sem("z_masked")
        x1_done = sem("x1_done")
        xc_hi_done, xc_lo_done, s_hi_done, s_lo_done = (
            sem(n) for n in ("xc_hi_done", "xc_lo_done", "s_hi_done", "s_lo_done"))
        w_eye, w_hi_done, w_split = sem("w_eye"), sem("w_hi_done"), sem("w_split")
        a_hi_done, a_split, ids_ready, own_ready = sem("a_hi_done"), sem("a_split"), sem("ids_ready"), sem("own_ready")
        gathered = sem("gathered")
        xhi_done, xlo_done, tab_hi, tab_lo = sem("xhi_done"), sem("xlo_done"), sem("tab_hi"), sem("tab_lo")
        idx_ready, idx_copied, m_ready, act_gathered = (
            sem(n) for n in ("idx_ready", "idx_copied", "m_ready", "act_gathered"))
        h_done, hb_done, hs_done, h2_done, hm_done, hhi_done, hlo_done = (
            sem(n) for n in ("h_done", "hb_done", "hs_done", "h2_done", "hm_done", "hhi_done", "hlo_done"))
        base_done, y_done, o_done = sem("base_done"), sem("y_done"), sem("o_done")

        block = ctx.enter_context(nc.Block())

        @block.sync
        def _(sp):
            sp.dma_start(par[:, :, :], params).then_inc(par_in, 16)
            sp.dma_start(tab[:, :, :], table).then_inc(table_in, 16)
            sp.dma_start(d_sb[:, :], d_row).then_inc(d_in, 16)
            sp.dma_start(a_raw[:, :, :], a_t).then_inc(a_in, 16)
            sp.dma_start(ids[:, :], ids_all).then_inc(ids_in, 16)
            sp.dma_start(row_c[:, :], row_of).then_inc(row_in, 16)
            sp.wait_ge(zeroed, 1)
            sp.dma_start(k_pad[:, 0:P], zero[:, :]).then_inc(pad_stored, 16)
            sp.dma_start(len_sb[:, :], length.to_broadcast((P, NB))).then_inc(len_in, 16)

            def load_x(h, s):
                sp.dma_start(x_in[:, s, :], x_conv[h]).then_inc(x_landed[s], 16)

            def load_strip(h, s):
                row = k_pad[bass.ds(h, 1), 1:1 + L]
                src = bass.AP(tensor=row.tensor, offset=row.offset, ap=[[1, P], [1, L]])
                sp.dma_start(strip[:, s, :].bitcast(F32), src).then_inc(strip_landed[s], 16)

            for s in range(XS):
                load_x(s, s)
            sp.dma_start(w_sb[:, :, :], w_t).then_inc(w_in, 16)
            sp.dma_start(bias_sb[:, :], bias.to_broadcast((P, L))).then_inc(bias_in, 16)

            sp.wait_ge(pad_stored, 16)
            sp.wait_ge(k_stored, 16)
            for s in range(XS):
                load_strip(s, s)

            def load_head(h, s):
                sp.wait_ge(xc_lo_done, h + (1 - XS))
                load_x(h, s)
                sp.wait_ge(conv_done, h + (1 - XS))
                load_strip(h, s)

            def load_chunk(n):
                sp.dma_start(x_t[:, n % TS, :], b_rows[n * BC:(n + 1) * BC, :]).then_inc(chunk_in[n % TS], 16)

            def store_chunk(n):
                sp.wait_ge(tab_lo, n + 1)
                for e, landed in enumerate((tab_hi_stored, tab_lo_stored)):
                    o = e * AD * R + n * BC
                    sp.dma_start(b_tab[o:o + BC, :], bt_hl[:, e, :].bitcast(F32)).then_inc(landed, 16)

            load_chunk(0)
            load_chunk(1)
            for h in range(XS, NU):
                if h in (G, 2 * G):
                    sp.wait_ge(k_stored, 16 * (h // G + 1))
                if h % XS == 1 and h // XS - 1 < NW:
                    n = h // XS - 1
                    store_chunk(n)
                    if n + TS < NW:
                        load_chunk(n + TS)
                load_head(h, h % XS)
            for h in range(NU, 3 * G):
                load_head(h, h % XS)
            sp.wait_ge(k_stored, 16 * NG)
            with sp.Fori(3 * G // XS, NH // XS) as lap:
                for s in range(XS):
                    load_head(lap * XS + s, s)

            def load_x_tile(t, s):
                sp.dma_start(x_t[:, s, :], x_tile[t]).then_inc(xt_landed[s], 16)

            def store(t, s):
                sp.wait_ge(o_done, t + 1)
                sp.dma_start(out[bass.ds(t * P, P), :], o_sb[:, s, :]).then_inc(stored[s], 16)

            for t in range(TS):
                load_x_tile(t, t)
            for t in range(TS, OS):
                sp.wait_ge(xlo_done, t + (1 - TS))
                load_x_tile(t, t % TS)
            with sp.Fori(1, NT // OS) as lap:
                for s in range(OS):
                    t = lap * OS + s
                    sp.wait_ge(xlo_done, t + (1 - TS))
                    load_x_tile(t, s % TS)
                    store(t - OS, s)
            for s in range(OS):
                store(NT - OS + s, s)
            for s in range(OS):
                sp.wait_ge(stored[s], 16 * (NT // OS))

        @block.gpsimd
        def _(pool):
            steps = [0]

            def link(ins):
                steps[0] += 1
                ins.then_inc(pool_step, 1)
                pool.wait_ge(pool_step, steps[0])

            g = nc.gpsimd
            link(g.memset(zero[:, :], 0.0))
            g.memset(row0[:, :], 0.0).then_inc(zeroed, 1)
            pool.wait_ge(zeroed, 1)
            g.memset(row0[:, 0:1], 1.0).then_inc(zeroed, 1)
            g.iota(pos, pattern=[[P, LC], [0, NB]], base=0, channel_multiplier=1).then_inc(pos_ready, 1)
            link(g.memset(eye[:, :], 0.0))
            link(g.affine_select(out=eye[:, :], in_=eye[:, :], compare_op=ALU.not_equal, fill=1.0,
                                 base=0, pattern=[[-1, P]], channel_multiplier=1))
            link(g.memset(own[:, :, :], 1.0))
            link(g.affine_select(out=own[:, :, :], in_=own[:, :, :], compare_op=ALU.is_ge, fill=0.0, base=0,
                                 pattern=[[-R, BT], [0, NH]], channel_multiplier=1))
            g.affine_select(out=own[:, :, :], in_=own[:, :, :], compare_op=ALU.is_ge, fill=0.0, base=R - 1,
                            pattern=[[R, BT], [0, NH]], channel_multiplier=-1).then_inc(own_ready, 1)
            pool.wait_ge(own_ready, 1)
            ai = par[:, 1, :]
            pool.wait_ge(par_in, 16)
            pool.wait_ge(ea_ready, 1)
            link(g.tensor_tensor(sm[:, 0, :], ea[:, :], ea[:, :], ALU.mult))
            link(g.tensor_tensor(sm[:, 1, :], ai, ai, ALU.mult))
            g.tensor_tensor(sm[:, 2, :], sm[:, 0, :], sm[:, 1, :], ALU.add).then_inc(den_ready, 1)
            pool.wait_ge(den_ready, 1)

            def twice(a):
                return a.unsqueeze(1).to_broadcast((P, 2, NH))

            link(g.tensor_tensor(sm[:, 4:6, :], par[:, 2:4, :], twice(ea[:, :]), ALU.mult))
            link(g.tensor_tensor(sm[:, 6:8, :], par[:, 4:6, :], twice(ai), ALU.mult))
            link(g.tensor_tensor(sm[:, 4, :], sm[:, 4, :], sm[:, 6, :], ALU.subtract))
            link(g.tensor_tensor(sm[:, 5, :], sm[:, 5, :], sm[:, 7, :], ALU.add))
            pool.wait_ge(den_ready, 2)
            link(g.tensor_tensor(sm[:, 4:6, :], sm[:, 4:6, :], twice(sm[:, 3, :]), ALU.mult))
            g.tensor_scalar(sm[:, 4:6, :], sm[:, 4:6, :], -2.0, None, ALU.mult).then_inc(m_ready, 1)
            pool.wait_ge(m_ready, 1)
            pool.wait_ge(table_in, 16)
            pool.wait_ge(zr_ready, 1)

            def exponents_of(h0, h1):
                n = h1 - h0
                g.tensor_tensor(mag[:, h0:h1, :], zr[:, h0:h1].unsqueeze(2).to_broadcast((P, n, NA + NC)),
                                tab[:, 0, NA:NF].unsqueeze(1).to_broadcast((P, n, NA + NC)),
                                ALU.mult).then_inc(exponents, 1)

            exponents_of(0, G)
            pool.wait_ge(exponents, 1)
            c, k, r, q = (sm[:, n, :] for n in range(8, 12))
            link(g.tensor_scalar(c, zr[:, :], -87.3, 88.0, ALU.max, ALU.min))
            link(g.tensor_scalar(k, c, LOG2_E, ROUND, ALU.mult, ALU.add))
            link(g.tensor_scalar(k, k, -ROUND, None, ALU.add))
            link(g.tensor_scalar(q, k, -LN2_HI, None, ALU.mult))
            link(g.tensor_tensor(r, q, c, ALU.add))
            link(g.tensor_scalar(q, k, -LN2_LO, None, ALU.mult))
            link(g.tensor_tensor(r, q, r, ALU.add))
            link(g.tensor_scalar(ez_i[:, :], k, 127.0, 2.0 ** 23, ALU.add, ALU.mult))
            link(g.tensor_scalar(q, r, 1 / 5040, 1 / 720, ALU.mult, ALU.add))
            for n in range(5, -1, -1):
                link(g.tensor_tensor(q, q, r, ALU.mult))
                link(g.tensor_scalar(q, q, 1 / math.factorial(n), None, ALU.add))
            g.tensor_tensor(ez[:, :], q, ez_i[:, :].bitcast(F32), ALU.mult).then_inc(ez_ready, 1)
            pool.wait_ge(ez_ready, 1)
            exponents_of(G, NH)
            pool.wait_ge(exponents, 2)
            pool.wait_ge(a_hi_done, 1)
            g.tensor_tensor(a_hl[:, :, 1, :], a_raw[:, :, :], a_hl[:, :, 0, :].bitcast(F32),
                            ALU.subtract).then_inc(a_split, 1)
            pool.wait_ge(a_split, 1)
            pool.wait_ge(w_in, 16)
            for c in range(LC):
                d = w_sb[:, c, c * P:(c + 1) * P]
                g.tensor_tensor(d, d, eye[:, :], ALU.add).then_inc(w_eye, 1)
            pool.wait_ge(w_eye, LC)

            def split_x(h, s):
                pool.wait_ge(xc_hi_done, h + 1)
                g.tensor_tensor(xp[:, s % CS, :, 1, :], x_in[:, s, :].rearrange("p (c n) -> p c n", c=LC),
                                xp[:, s % CS, :, 0, :].bitcast(F32), ALU.subtract).then_inc(xc_lo_done, 1)

            for h in range(NU):
                split_x(h, h % XS)
                if h % XS == 1 and h // XS < NW:
                    n = h // XS
                    pool.wait_ge(tab_hi, n + 1)
                    g.tensor_tensor(bt_hl[:, 1, :], x_t[:, n % TS, :], bt_hl[:, 0, :].bitcast(F32),
                                    ALU.subtract).then_inc(tab_lo, 1)
                if h == 7:
                    pool.wait_ge(ids_in, 16)
                    pool.wait_ge(row_in, 16)
                    link(g.tensor_copy(id_f[:, 1, :], ids[:, :]))
                    link(g.tensor_scalar(id_f[:, 0, :], id_f[:, 1, :], 0.0, float(AD), ALU.is_lt, ALU.mult))
                    link(g.tensor_tensor(id_f[:, 1, :], id_f[:, 1, :], id_f[:, 0, :], ALU.add))
                    link(g.tensor_scalar(id_f[:, 0, :], id_f[:, 1, :], 0.0, float(AD - 1), ALU.max, ALU.min))
                    g.tensor_copy(ids[:, :], id_f[:, 0, :]).then_inc(ids_ready, 1)
                    pool.wait_ge(ids_ready, 1)
                    g.tensor_scalar(b_idx[:, :], ids[:, NB:NB + NT], float(R), row_c[:, :], ALU.mult,
                                    ALU.add).then_inc(idx_ready, 1)
                    pool.wait_ge(idx_ready, 1)

            def split_w(n):
                pool.wait_ge(w_hi_done, n + 1)
                g.tensor_tensor(w_lo[:, bass.ds(n, 1), :], w_sb[:, bass.ds(n, 1), :],
                                w_hi[:, bass.ds(n, 1), :].bitcast(F32), ALU.subtract).then_inc(w_split, 1)

            split_w(0)
            with pool.Fori(NU // XS, NH // XS) as lap:
                for s in range(XS):
                    split_x(lap * XS + s, s)
                split_w(lap + (1 - NU // XS))

            def gather(t, s):
                for q in range(QA, BT):
                    i = pool.value_load(ids[0:1, bass.ds(t * BT + q, 1)], min_val=0, max_val=AD - 1)
                    src = a_hl[:, bass.ds(i, 1), :, :].bitcast(F32).rearrange("p o e (c r) -> p (o e) c r", c=LC)
                    last = g.tensor_copy(ag[:, s, :, :, q, :].rearrange("p c e r -> p e c r"), src)
                last.then_inc(gathered, 1)

            def index_b(t, s):
                g.tensor_copy(b_now[:, s:s + 1], b_idx[:, bass.ds(t, 1)]).then_inc(idx_copied, 1)
                pool.wait_ge(idx_copied, t + 1)

            def gather_b(s):
                g.indirect_dma_start(out=b_hl[:, s, :].bitcast(F32), out_offset=None, in_=b_tab,
                                     in_offset=bass.IndirectOffsetOnAxis(ap=b_now[:, s:s + 1], axis=0)
                                     ).then_inc(b_landed[s], 16)

            pool.wait_ge(tab_hi_stored, 16 * NW)
            pool.wait_ge(tab_lo_stored, 16 * NW)
            pool.wait_ge(idx_ready, 1)
            pool.wait_ge(w_split, NW)
            gather(0, 0)
            gather(1, 1)
            pool.wait_ge(conv_done, NH)
            for t in range(BS):
                index_b(t, t)
                gather_b(t)
            for t in range(TS, BS):
                pool.wait_ge(h_done, t + (1 - TS))
                gather(t, t % TS)
            with pool.Fori(1, NT // BS) as lap:
                for s in range(BS):
                    t = lap * BS + s
                    pool.wait_ge(y_done, t + (1 - BS))
                    index_b(t, s)
                    pool.wait_ge(h_done, t + (1 - TS))
                    gather(t, s % TS)
                    gather_b(s)

        @block.scalar
        def _(act):
            act.wait_ge(par_in, 16)
            nc.scalar.activation(ea[:, :], par[:, 0, :], ACT.Exp).then_inc(ea_ready, 1)
            act.wait_ge(exponents, 1)
            nc.scalar.activation(mag[:, 0:G, :], mag[:, 0:G, :], ACT.Exp).then_inc(mags, 1)
            act.wait_ge(a_in, 16)
            nc.scalar.activation(a_hl[:, :, 0, :], a_raw[:, :, :], ACT.Copy).then_inc(a_hi_done, 1)

            def group_sines(k):
                act.wait_ge(reduced, k + 1)
                nc.scalar.activation(sines[:, :, :], red[:, :, :], ACT.Sin).then_inc(sines_ready, 1)

            def group_store(k):
                s = k % KS
                act.wait_ge(k_done, k + 1)
                if k >= KS:
                    act.wait_ge(k_stored, 16 * (k - 1))
                nc.scalar.activation(k_sb[:, s, :], k_ps[0:NA, s, 0:G * NC], ACT.Copy).then_inc(k_copied, 1)
                act.wait_ge(k_copied, k + 1)
                if k >= 1:
                    act.wait_ge(k_stored, 16 * k)
                act.dma_start(k_pad[k * G:(k + 1) * G, P:PAD].rearrange("h (a c) -> a h c", a=NA),
                              k_sb[:, s, :].rearrange("a (h c) -> a h c", c=NC)).then_inc(k_stored, 16)

            def split_x(h, s, lap, first):
                act.wait_ge(x_landed[s], 16 * (lap + 1))
                if not first:
                    act.wait_ge(conv_done, h + (1 - CS))
                act.activation(xp[:, s % CS, :, 0, :], x_in[:, s, :].rearrange("p (c n) -> p c n", c=LC),
                               ACT.Copy).then_inc(xc_hi_done, 1)

            def split_strip(h, s, lap):
                act.wait_ge(strip_landed[s], 16 * (lap + 1))
                act.activation(s_hi[:, s % CS, :], strip[:, s, :].bitcast(F32), ACT.Copy).then_inc(s_hi_done, 1)

            def split_w(n):
                act.activation(w_hi[:, bass.ds(n, 1), :], w_sb[:, bass.ds(n, 1), :], ACT.Copy).then_inc(w_hi_done, 1)

            group_sines(0)
            act.wait_ge(angle_ready, 1)
            nc.scalar.activation(cs[:, :, :], an[:, 0, :, :], ACT.Sin).then_inc(cs_ready, 1)
            split_x(0, 0, 0, True)
            split_x(1, 1, 0, True)
            group_store(0)
            act.wait_ge(exponents, 2)
            nc.scalar.activation(mag[:, G:NH, :], mag[:, G:NH, :], ACT.Exp).then_inc(mags, 1)
            group_sines(1)
            for h in range(NU):
                if h >= 2:
                    split_x(h, h % XS, h // XS, h < CS)
                split_strip(h, h % XS, h // XS)
                if h in (1, G + 3, 2 * G + 3):
                    group_store((h + G - 1) // G)
                if h in (6, G + 6):
                    group_sines(h // G + 2)
                if h % XS == 1 and h // XS < NW:
                    n = h // XS
                    act.wait_ge(chunk_in[n % TS], 16 * (n // TS + 1))
                    if n:
                        act.wait_ge(tab_hi_stored, 16 * n)
                        act.wait_ge(tab_lo_stored, 16 * n)
                    act.activation(bt_hl[:, 0, :], x_t[:, n % TS, :], ACT.Copy).then_inc(tab_hi, 1)
            act.wait_ge(w_eye, LC)
            split_w(0)
            with act.Fori(NU // XS, NH // XS) as lap:
                split_w(lap + (1 - NU // XS))
                for s in range(XS):
                    split_x(lap * XS + s, s, lap, False)
                    split_strip(lap * XS + s, s, lap)

            def gather(t, s):
                for q in range(QA):
                    i = act.value_load(ids[0:1, bass.ds(t * BT + q, 1)], min_val=0, max_val=AD - 1)
                    src = a_hl[:, bass.ds(i, 1), :, :].bitcast(F32).rearrange("p o e (c r) -> p (o e) c r", c=LC)
                    for e in range(2):
                        last = act.activation(ag[:, s, :, e, q, :], src[:, e, :, :], ACT.Copy)
                last.then_inc(act_gathered, 1)

            def step(i, s):
                known = isinstance(i, int)
                if not known or i + 2 < NT:
                    act.wait_ge(x1_done, i + 3)
                    if not known or i + 2 >= HS:
                        act.wait_ge(base_done, i + (3 - HS))
                    act.activation(xp[:, (s + 2) % HS, :, 0, :], x_t[:, s % TS, :].rearrange("p (c n) -> p c n", c=LC),
                                   ACT.Copy).then_inc(xhi_done, 1)
                if not known or 0 <= i + 1:
                    b = (s + 1) % TS
                    act.wait_ge(h_done, i + 2)
                    act.activation(h_b[:, b, :], h_ps[BR:P, b, 0:2 * P], ACT.Copy).then_inc(hb_done, 1)
                    if not known or i + 3 < NT:
                        gather(i + 3, b)
                    act.wait_ge(hm_done, i + 2)
                    if not known or i + 1 >= TS:
                        act.wait_ge(y_done, i + (2 - TS))
                    for o in (0, BR):
                        act.activation(h_hi[o:o + BR, b, :], h_m[:, b, :], ACT.Copy).then_inc(hhi_done, 1)

            act.wait_ge(ids_ready, 1)
            act.wait_ge(a_split, 1)
            gather(0, 0)
            gather(1, 1)
            for i in range(-2, 2):
                step(i, i % OS)
            with act.Fori(0, NT // OS - 2) as lap:
                for s in range(2, OS + 2):
                    step(lap * OS + s, s)
            for i in range(NT - OS - 2, NT - 1):
                step(i, i % OS)

        @block.vector
        def _(dve):
            steps = [0]

            def link(ins):
                steps[0] += 1
                ins.then_inc(dve_step, 1)
                dve.wait_ge(dve_step, steps[0])

            V = nc.vector
            def exp(dst, x):
                c, k, r, q = (ex[:, n, :] for n in range(4))
                link(V.tensor_scalar(c, x, -87.3, 88.0, ALU.max, ALU.min))
                link(V.tensor_scalar(k, c, LOG2_E, ROUND, ALU.mult, ALU.add))
                link(V.tensor_scalar(k, k, -ROUND, None, ALU.add))
                link(V.scalar_tensor_tensor(r, k, -LN2_HI, c, ALU.mult, ALU.add))
                link(V.scalar_tensor_tensor(r, k, -LN2_LO, r, ALU.mult, ALU.add))
                link(V.tensor_scalar(ex_i[:, :], k, 127.0, 2.0 ** 23, ALU.add, ALU.mult))
                link(V.tensor_scalar(q, r, 1 / 5040, None, ALU.mult))
                for n in range(6, 0, -1):
                    link(V.scalar_tensor_tensor(q, q, 1 / math.factorial(n), r, ALU.add, ALU.mult))
                return V.scalar_tensor_tensor(dst, q, 1.0, ex_i[:, :].bitcast(F32), ALU.add, ALU.mult)

            dve.wait_ge(par_in, 16)
            link(exp(dt[:, :], par[:, 6, :]))
            dve.wait_ge(ea_ready, 1)
            V.scalar_tensor_tensor(zr[:, :], ea[:, :], -1.0, dt[:, :], ALU.mult, ALU.mult).then_inc(zr_ready, 1)
            link(V.tensor_tensor(zi[:, :], par[:, 1, :], dt[:, :], ALU.mult))

            def small_angles():
                for n, turns in ((0, 0.25), (1, 0.0)):
                    V.tensor_scalar(an[:, 1, n, :], zi[:, :], 1 / (2 * math.pi), turns, ALU.mult,
                                    ALU.add).then_inc(dve_step, 1)
                steps[0] += 2
                dve.wait_ge(dve_step, steps[0])
                turns, angle = an[:, 1, :, :], an[:, 0, :, :]
                link(V.tensor_scalar(turns, turns, ROUND, -ROUND, ALU.add, ALU.add))
                link(V.scalar_tensor_tensor(angle, turns, -TWO_PI_HI, zi[:, :].unsqueeze(1).to_broadcast((P, 2, NH)),
                                            ALU.mult, ALU.add))
                link(V.scalar_tensor_tensor(angle, turns, -TWO_PI_LO, angle, ALU.mult, ALU.add))
                link(V.tensor_scalar(an[:, 0, 0, :], an[:, 0, 0, :], math.pi / 2, None, ALU.add))
                V.tensor_scalar(angle, angle, -PI, PI, ALU.max, ALU.min).then_inc(angle_ready, 1)

            dve.wait_ge(den_ready, 1)
            V.reciprocal(sm[:, 3, :], sm[:, 2, :]).then_inc(den_ready, 1)

            cr, ci = sm[:, 14, :], sm[:, 15, :]

            def ct():
                dve.wait_ge(ez_ready, 1)
                dve.wait_ge(cs_ready, 1)
                link(V.tensor_tensor(cs[:, :, :], cs[:, :, :], ez[:, :].unsqueeze(1).to_broadcast((P, 2, NH)), ALU.mult))
                link(V.tensor_scalar(cs[:, 0, :], cs[:, 0, :], -1.0, None, ALU.add))
                dve.wait_ge(m_ready, 1)
                link(V.tensor_tensor(cs_m[:, 0:2, :], cs[:, :, :], sm[:, 4, :].unsqueeze(1).to_broadcast((P, 2, NH)),
                                     ALU.mult))
                link(V.tensor_tensor(cs_m[:, 2:4, :], cs[:, :, :], sm[:, 5, :].unsqueeze(1).to_broadcast((P, 2, NH)),
                                     ALU.mult))
                link(V.tensor_tensor(cr, cs_m[:, 0, :], cs_m[:, 3, :], ALU.subtract))
                link(V.tensor_tensor(ci, cs_m[:, 1, :], cs_m[:, 2, :], ALU.add))

            l_col = tab[:, 0, :].unsqueeze(1).to_broadcast((P, G, NF))
            turn_col = tab[:, 1, :].unsqueeze(1).to_broadcast((P, G, NF))
            phase_col = tab[:, 2, :].unsqueeze(1).to_broadcast((P, G, NF))

            def group(k):
                hs, s = slice(k * G, (k + 1) * G), k % KS
                wide = lambda a, n: a[:, hs].unsqueeze(2).to_broadcast((P, G, n))

                def angles():
                    link(V.tensor_tensor(ang[:, :, :], wide(zi, NF), l_col, ALU.mult))

                def whole_turns():
                    link(V.scalar_tensor_tensor(trn[:, :, :], ang[:, :, :], 1 / (2 * math.pi), turn_col,
                                                ALU.mult, ALU.add))
                    link(V.tensor_scalar(trn[:, :, :], trn[:, :, :], ROUND, -ROUND, ALU.add, ALU.add))

                def reduce_hi():
                    if k:
                        dve.wait_ge(sines_ready, k)
                    link(V.scalar_tensor_tensor(red[:, :, :], trn[:, :, :], -TWO_PI_HI, ang[:, :, :],
                                                ALU.mult, ALU.add))

                def reduce_lo():
                    link(V.scalar_tensor_tensor(red[:, :, :], trn[:, :, :], -TWO_PI_LO, red[:, :, :],
                                                ALU.mult, ALU.add))

                def bound():
                    link(V.tensor_tensor(red[:, :, :], red[:, :, :], phase_col, ALU.add))
                    V.tensor_scalar(red[:, :, :], red[:, :, :], -PI, PI, ALU.max, ALU.min).then_inc(reduced, 1)

                def multiply():
                    dve.wait_ge(sines_ready, k + 1)
                    if k >= KS:
                        dve.wait_ge(k_done, k + 1 - KS)
                    link(V.tensor_tensor(gg[:, s, :, :], sines[:, :, 0:NA], wide(cr, NA), ALU.mult))
                    link(V.tensor_tensor(g2[:, :, :], sines[:, :, NA:2 * NA], wide(ci, NA), ALU.mult))
                    link(V.tensor_tensor(gg[:, s, :, :], gg[:, s, :, :], g2[:, :, :], ALU.add))

                def scale():
                    dve.wait_ge(mags, 1 if k == 0 else 2)
                    V.tensor_tensor(gg[:, s, :, :], gg[:, s, :, :], mag[:, hs, 0:NA], ALU.mult).then_inc(factors, 1)
                    V.tensor_tensor(ee[:, s, :, :], sines[:, :, 2 * NA:NF], mag[:, hs, NA:NA + NC],
                                    ALU.mult).then_inc(factors, 1)

                return [angles, whole_turns, reduce_hi, reduce_lo, bound, multiply, scale]

            dve.wait_ge(table_in, 16)
            for k in range(2):
                todo = group(k)
                if k == 0:
                    todo[5:5] = [small_angles, ct]
                for do in todo:
                    do()
                if k == 0:
                    dve.wait_ge(pos_ready, 1)
                    dve.wait_ge(len_in, 16)
                    link(V.tensor_tensor(mask[:, :, :], pos,
                                         len_sb[:, :].unsqueeze(1).to_broadcast((P, LC, NB)), ALU.is_lt))

            m2 = mask[:, :, :].rearrange("p c b -> p (c b)")

            def split(h, s):
                dve.wait_ge(s_hi_done, h + 1)
                V.tensor_tensor(strip[:, s, :], strip[:, s, :].bitcast(F32), s_hi[:, s % CS, :].bitcast(F32),
                                ALU.subtract).then_inc(s_lo_done, 1)

            def head(h, s):
                dve.wait_ge(conv_done, h + 1)
                V.tensor_tensor(z_all[:, :, :, bass.ds(h, 1)].rearrange("p c b o -> p (c b o)"),
                                z_ps[:, s % ZS, :], m2, ALU.mult).then_inc(z_masked, 1)

            beside = {o + j: do for o, k in ((0, 2), (G, 3))
                      for j, do in zip((0, 1, 2, 3, 4, 6, 7), group(k))}
            for h in range(NU):
                split(h, h % XS)
                if h >= 2:
                    head(h - 2, (h - 2) % XS)
                if h in beside:
                    beside[h]()
            with dve.Fori(NU // XS, NH // XS) as lap:
                for s in range(XS):
                    split(lap * XS + s, s)
                    head(lap * XS + (s - 2), (s - 2) % XS)
            for h in (NH - 2, NH - 1):
                head(h, h % XS)

            def x1_of(t, s, lap):
                dve.wait_ge(xt_landed[s % TS], 16 * (lap + 1))
                xt = x_t[:, s % TS, :].rearrange("p (c n) -> p c n", c=LC)
                V.tensor_tensor(xt, xt, z_all[:, :, bass.ds(t * BT, BT), :].rearrange("p c b h -> p c (b h)"),
                                ALU.add).then_inc(x1_done, 1)

            def step(i, s, lap):
                known = isinstance(i, int)

                def there(t):
                    return not known or 0 <= t < NT

                if there(i - 1):
                    dve.wait_ge(y_done, i)
                    if not known or i - 1 >= OS:
                        dve.wait_ge(stored[(s - 1) % OS], 16 * (lap + (s - 1) // OS))
                    V.tensor_tensor(o_sb[:, (s - 1) % OS, :], y_ps[:, (s - 1) % TS, :], bias_sb[:, :],
                                    ALU.add).then_inc(o_done, 1)
                b = (s + 1) % TS
                if there(i + 1):
                    dve.wait_ge(hb_done, i + 2)
                    V.tensor_tensor(h_s[:, b, :], h_ps[0:BR, b, 0:2 * P], h_b[:, b, :], ALU.add).then_inc(hs_done, 1)
                    dve.wait_ge(hs_done, i + 2)
                    V.tensor_tensor(h_s[:, b, 0:P], h_s[:, b, 0:P], h_s[:, b, P:2 * P], ALU.add).then_inc(h2_done, 1)
                    dve.wait_ge(h2_done, i + 2)
                    V.tensor_tensor(h_m[:, b, :], h_s[:, b, 0:P], own[:, :, :].rearrange("p b h -> p (b h)"),
                                    ALU.mult).then_inc(hm_done, 1)
                if there(i + 2):
                    x = (s + 2) % HS
                    dve.wait_ge(xhi_done, i + 3)
                    V.tensor_tensor(xp[:, x, :, 1, :], x_t[:, s % TS, :].rearrange("p (c n) -> p c n", c=LC),
                                    xp[:, x, :, 0, :].bitcast(F32), ALU.subtract).then_inc(xlo_done, 1)
                if there(i + 1):
                    dve.wait_ge(hhi_done, 2 * i + 4)
                    V.tensor_tensor(h_lo[:, b, :], h_m[:, b, :], h_hi[0:BR, b, :].bitcast(F32),
                                    ALU.subtract).then_inc(hlo_done, 1)
                if there(i + 3):
                    t = s + 3
                    x1_of(i + 3, t, lap * (OS // TS) + t // TS)

            dve.wait_ge(own_ready, 1)
            dve.wait_ge(bias_in, 16)
            dve.wait_ge(z_masked, NH)
            for i in range(-3, OS + 1):
                step(i, i % OS, i // OS)
            with dve.Fori(1, NT // OS - 1) as lap:
                for s in range(1, OS + 1):
                    step(lap * OS + s, s, lap)
            for i in range(NT - OS + 1, NT + 1):
                step(i, i % OS, i // OS)

        @block.tensor
        def _(pe):
            pe.wait_ge(d_in, 16)
            pe.wait_ge(zeroed, 2)

            def group_d(k):
                if k >= KS:
                    pe.wait_ge(k_copied, k + 1 - KS)
                nc.tensor.matmul(k_ps[0:NA, k % KS, 0:G * NC], row0[:, :], d_sb[:, k * G * NC:(k + 1) * G * NC],
                                 start=True, stop=False)

            def group(k):
                s = k % KS
                pe.wait_ge(factors, 2 * (k + 1))
                for i in range(G):
                    last = nc.tensor.matmul(k_ps[0:NA, s, i * NC:(i + 1) * NC], gg[:, s, i, :], ee[:, s, i, :],
                                            start=False, stop=(i == G - 1))
                last.then_inc(k_done, 1)

            def head(h, s, first):
                pe.wait_ge(xc_lo_done, h + 1)
                pe.wait_ge(s_lo_done, h + 1)
                if not first:
                    pe.wait_ge(z_masked, h + (1 - ZS))
                terms = [(m, t, e) for m in range(LC) for t, e in ((s_hi, 0), (s_hi, 1), (strip, 0))]
                for n, (m, t, e) in enumerate(terms):
                    last = nc.tensor.matmul(z_ps[:, s % ZS, m * P:L], t[:, s % CS, m * P:(m + 1) * P],
                                            xp[:, s % CS, 0:LC - m, e, :], start=(n == 0), stop=(n == len(terms) - 1))
                last.then_inc(conv_done, 1)

            group_d(0)
            group_d(1)
            group(0)
            group(1)
            for h in range(NU):
                head(h, h % XS, h < ZS)
                if h in (G - 1, 2 * G - 1):
                    group_d(h // G + 2)
                    group(h // G + 2)
            with pe.Fori(NU // XS, NH // XS) as lap:
                for s in range(XS):
                    head(lap * XS + s, s, False)

            def tile_h(t, s, first):
                pe.wait_ge(gathered, t + 1)
                pe.wait_ge(act_gathered, t + 1)
                pe.wait_ge(xlo_done, t + 1)
                if not first:
                    pe.wait_ge(hs_done, t + (1 - TS))
                for c in range(LC):
                    last = nc.tensor.matmul(h_ps[:, s % TS, 0:2 * P],
                                            ag[:, s % TS, c, :, :, :].rearrange("p e b r -> p (e b r)"),
                                            xp[:, s % HS, c, :, :].rearrange("p e n -> p (e n)"),
                                            start=(c == 0), stop=(c == LC - 1))
                last.then_inc(h_done, 1)

            def tile_y(t, s, lap, first):
                b = s % TS
                if not first:
                    pe.wait_ge(o_done, t + (1 - TS))
                terms = [(c, e, w) for c in range(LC) for e, w in ((0, w_hi), (0, w_lo), (1, w_hi))]
                for n, (c, e, w) in enumerate(terms):
                    last = nc.tensor.matmul(y_ps[:, b, :], xp[:, s % HS, c, e, :], w[:, c, :], start=(n == 0), stop=False)
                last.then_inc(base_done, 1)
                pe.wait_ge(b_landed[s % BS], 16 * (lap + 1))
                pe.wait_ge(hlo_done, t + 1)
                nc.tensor.matmul(y_ps[:, b, :], h_hi[:, b, :], b_hl[:, s % BS, :], start=False, stop=False)
                nc.tensor.matmul(y_ps[:, b, :], h_lo[:, b, :], b_hl[0:BR, s % BS, :],
                                 start=False, stop=True).then_inc(y_done, 1)

            pe.wait_ge(z_masked, NH)
            pe.wait_ge(w_split, NW)
            tile_h(0, 0, True)
            for t in range(OS):
                tile_h(t + 1, t + 1, t + 1 < TS)
                tile_y(t, t, 0, t < TS)
            with pe.Fori(1, NT // OS - 1) as lap:
                for s in range(OS):
                    t = lap * OS + s
                    tile_h(t + 1, s + 1, False)
                    tile_y(t, s, lap, False)
            for t in range(NT - OS, NT):
                if t + 1 < NT:
                    tile_h(t + 1, t + 1, False)
                tile_y(t, t, NT // OS - 1, False)


def kernel(**inputs):
    import numpy as np
    import concourse.bacc as bacc
    from concourse.bass_utils import run_bass_kernel_spmd

    g = {k: np.asarray(v) for k, v in inputs.items()}

    def both(a):
        return np.concatenate([a.T, a.T], axis=0)

    c = g["L0_cond_C"]
    params = np.stack([both(g["L0_cond_log_A_real"]), both(g["L0_cond_A_imag"]), both(c[..., 0]), both(c[..., 1]),
                       both(c[..., 1]), both(c[..., 0]),
                       np.broadcast_to(g["L0_cond_log_dt"][None, :], (P, NH))], axis=1)
    table = np.zeros((P, 3, NF), np.float32)
    table[:, 0] = np.concatenate([NC * np.arange(NA), NC * np.arange(NA), np.arange(NC)])
    for half, phases in enumerate(((0.25, 0.5, 0.25), (0.0, 0.25, 0.5))):
        turns = np.repeat(phases, (NA, NA, NC))
        table[half * NS:(half + 1) * NS, 1] = turns
        table[half * NS:(half + 1) * NS, 2] = 2 * math.pi * turns
    ids = g["itok_B_6_15"]
    d_row = np.zeros((NH, NC), g["L0_cond_D"].dtype)
    d_row[:, 0] = g["L0_cond_D"]
    arrays = {
        "x_conv": g["x"].transpose(1, 2, 0).reshape(NH, LC, P, NB).transpose(0, 2, 1, 3)[:, ::-1].reshape(NH, P, L),
        "x_tile": g["x"].reshape(NT, P, LC, P).transpose(0, 3, 2, 1).reshape(NT, P, L),
        "params": params,
        "table": table,
        "d_row": d_row.reshape(1, NH * NC),
        "length": g["itok_B_78_3631"].reshape(1, NB),
        "ids_all": np.concatenate([np.broadcast_to(ids, (P, NB)), np.broadcast_to(
            ids.reshape(1, NT, BT, 1), (2, NT, BT, R)).transpose(0, 2, 3, 1).reshape(P, NT)], axis=1),
        "w_t": g["L1_cond_base_weight"].T.reshape(LC, P, L).transpose(1, 0, 2),
        "bias": g["L1_cond_base_bias"].reshape(1, L),
        "a_t": g["L1_cond_lora_A_w"].reshape(AD, R, LC, P).transpose(3, 0, 2, 1).reshape(P, AD, LC * R),
        "b_rows": g["L1_cond_lora_B_w"].transpose(0, 2, 1).reshape(AD * R, L),
        "row_of": (AD * R * (np.arange(P) // BR) + np.arange(P) % R).astype(np.float32).reshape(P, 1),
    }
    arrays = {k: np.ascontiguousarray(v) for k, v in arrays.items()}
    nc = bacc.Bacc("TRN2", target_bir_lowering=False, num_devices=1)
    args = [nc.dram_tensor(k, a.shape, mybir.dt.from_np(a.dtype), kind="ExternalInput").ap()
            for k, a in arrays.items()]
    args.append(nc.dram_tensor("out", (NB * NH, L), F32, kind="ExternalOutput").ap())
    build(nc, *args)
    r = run_bass_kernel_spmd(nc, [arrays], core_ids=[0])
    return r.results[0]["out"].reshape(NB, NH, L)
```

```python
import math
from contextlib import ExitStack

import concourse.bass as bass
from concourse import mybir

F32 = mybir.dt.float32
F32R = mybir.dt.float32r
I32 = mybir.dt.int32
ALU = mybir.AluOpType
ACT = mybir.ActivationFunctionType

P = 128
NB, NH, L = 128, 32, 512
NS = 64
LC = L // P
AD, R = 32, 16
NA, NC = 16, 32
BT = P // NH
NT = NB // BT
BR = BT * R
PAD = P + L
assert NA * NC == L and 2 * NS == P

TWO_PI_HI = 6.28125
TWO_PI_LO = 2 * math.pi - TWO_PI_HI
PI = 3.1415925
ROUND = 1.5 * 2.0 ** 23

G = 8
NG = NH // G
NF = 2 * NA + NC
LOG2_E = 1 / math.log(2)
LN2_HI = 0.693359375
LN2_LO = math.log(2) - LN2_HI

XS = 4
CS = 4
ZS = 4
KS = 2
XT = 4
TS = 2
HS = CS
BS = XS
OS = XS
AHEAD = 6
EARLY = NH - 2
NW = 4
NU = 24
K_AFTER = {1: 0, 2: 8, 3: 16}
STEPS_AT = {2: (0, 1, 2, 3, 4, 6, 7), 3: (8, 9, 10, 11, 13, 15, 16)}
QA = 2
BC = AD * R // NW
assert G * NF == TS * 2 * P and EARLY % XS == TS
assert NU == 3 * G and BC == P and NW == LC == XT and 2 * BR == P


def build(nc, x_conv, x_tile, params, table, d_row, length, ids_all, w_t, bias, a_t, b_rows, row_of, out):
    ctx = ExitStack()
    with ctx:
        def sb(name, shape, dt=F32):
            return ctx.enter_context(nc.sbuf_tensor(name, shape, dt))

        def pb(name, shape):
            return ctx.enter_context(nc.psum_tensor(name, shape, F32))

        def sem(name):
            return ctx.enter_context(nc.semaphore(name))

        k_pad = nc.dram_tensor("k_pad", (NH, PAD), F32, kind="Internal").ap()
        b_tab = nc.dram_tensor("b_tab", (2 * AD * R, L), F32, kind="Internal").ap()

        par = sb("par", [P, 7, NH])
        tab = sb("tab", [P, 3, NF])
        dt = sb("dt", [P, NH])
        ea = sb("ea", [P, NH])
        zr = sb("zr", [P, NH])
        zi = sb("zi", [P, NH])
        ez = sb("ez", [P, NH])
        ex = sb("ex", [P, 4, NH])
        ex_i = sb("ex_i", [P, NH], I32)
        ez_i = sb("ez_i", [P, NH], I32)
        an = sb("an", [P, 2, 2, NH])
        cs = sb("cs", [P, 2, NH])
        cs_m = sb("cs_m", [P, 4, NH])
        sm = sb("sm", [P, 16, NH])
        mag = sb("mag", [P, NH, NA + NC])
        ang = sb("ang", [P, G, NF])
        trn = sb("trn", [P, G, NF])
        red = sb("red", [P, G, NF])
        sines = sb("sines", [P, G, NF])
        gg = sb("gg", [P, KS, G, NA])
        g2 = sb("g2", [P, G, NA])
        ee = sb("ee", [P, KS, G, NC])
        k_sb = sb("k_sb", [NA, KS, G * NC])
        d_sb = sb("d_sb", [1, NH])
        row0 = sb("row0", [1, NA])
        zero = sb("zero", [NH, P])
        len_sb = sb("len_sb", [P, NB], I32)
        mask = sb("mask", [P, LC, NB])
        pos = mask[:, :, :].bitcast(I32)
        x_in = sb("x_in", [P, XS, L])
        strip = sb("strip", [P, XS, L], F32R)
        xp = sb("xp", [P, CS, LC, 2, P], F32R)
        s_hi = sb("s_hi", [P, CS, L], F32R)
        z_all = sb("z_all", [P, LC, NB, NH])
        w_sb = sb("w_sb", [P, LC, L])
        w_hi = sb("w_hi", [P, LC, L], F32R)
        w_lo = sb("w_lo", [P, LC, L], F32R)
        eye = sb("eye", [P, P])
        a_raw = sb("a_raw", [P, AD, LC * R])
        a_hl = sb("a_hl", [P, AD, 2, LC * R], F32R)
        ids = sb("ids", [P, NB + NT], I32)
        id_f = sb("id_f", [P, 2, NB + NT])
        row_c = sb("row_c", [P, 1])
        b_now = sb("b_now", [P, XS], I32)
        b_idx = sb("b_idx", [P, NT], I32)
        ag = sb("ag", [P, TS, LC, 2, BT, R], F32R)
        own = sb("own", [BR, BT, NH])
        bias_sb = sb("bias_sb", [P, L])
        x_t = sb("x_t", [P, XT, L])
        b_hl = strip
        o_sb = x_in
        h_b = ang[0:BR, :, :].rearrange("p g f -> p (g f)").rearrange("p (t m) -> p t m", t=TS)
        h_s = trn[0:BR, :, :].rearrange("p g f -> p (g f)").rearrange("p (t m) -> p t m", t=TS)
        h_m = sb("h_m", [BR, TS, P])
        h_hi = sb("h_hi", [P, TS, P], F32R)
        h_lo = sb("h_lo", [BR, TS, P], F32R)

        k_ps = pb("k_ps", [P, KS, L])
        z_ps = pb("z_ps", [P, ZS, L])
        y_ps = pb("y_ps", [P, TS, L])
        h_ps = z_ps

        par_in, table_in, d_in, len_in, ids_in = (sem(n) for n in ("par_in", "table_in", "d_in", "len_in", "ids_in"))
        w_in, a_in, bias_in = sem("w_in"), sem("a_in"), sem("bias_in")
        x_landed = [sem(f"x_landed{s}") for s in range(XS)]
        strip_landed = [sem(f"strip_landed{s}") for s in range(XS)]
        xt_landed = [sem(f"xt_landed{s}") for s in range(XT)]
        chunk_in = [sem(f"chunk_in{n}") for n in range(NW)]
        row_in, tab_hi_stored, tab_lo_stored = sem("row_in"), sem("tab_hi_stored"), sem("tab_lo_stored")
        b_landed = [sem(f"b_landed{s}") for s in range(BS)]
        stored = [sem(f"stored{s}") for s in range(OS)]
        k_stored, pad_stored = sem("k_stored"), sem("pad_stored")
        pool_step, dve_step = sem("pool_step"), sem("dve_step")
        pos_ready, zeroed, ea_ready, zr_ready, ez_ready = (
            sem(n) for n in ("pos_ready", "zeroed", "ea_ready", "zr_ready", "ez_ready"))
        den_ready, exponents, mags, angle_ready, cs_ready, ct_ready = (
            sem(n) for n in ("den_ready", "exponents", "mags", "angle_ready", "cs_ready", "ct_ready"))
        reduced, sines_ready, factors, k_done, k_copied = (
            sem(n) for n in ("reduced", "sines_ready", "factors", "k_done", "k_copied"))
        conv_done, z_masked = sem("conv_done"), sem("z_masked")
        x1_done, x1_early, xhi_early, xlo_early = (sem(n) for n in ("x1_done", "x1_early", "xhi_early", "xlo_early"))
        xc_hi_done, xc_lo_done, s_hi_done, s_lo_done = (
            sem(n) for n in ("xc_hi_done", "xc_lo_done", "s_hi_done", "s_lo_done"))
        eye_ready, w_eye, w_hi_done, w_split = sem("eye_ready"), sem("w_eye"), sem("w_hi_done"), sem("w_split")
        a_hi_done, a_split, ids_ready, own_ready = sem("a_hi_done"), sem("a_split"), sem("ids_ready"), sem("own_ready")
        gathered = sem("gathered")
        xhi_done, xlo_done, tab_hi, tab_lo = sem("xhi_done"), sem("xlo_done"), sem("tab_hi"), sem("tab_lo")
        idx_ready, idx_copied, m_ready, act_gathered = (
            sem(n) for n in ("idx_ready", "idx_copied", "m_ready", "act_gathered"))
        h_done, hb_done, hs_done, h2_done, hm_done, hhi_done, hlo_done = (
            sem(n) for n in ("h_done", "hb_done", "hs_done", "h2_done", "hm_done", "hhi_done", "hlo_done"))
        base_done, y_done, o_done = sem("base_done"), sem("y_done"), sem("o_done")

        def in_chunks(a):
            return a.rearrange("p (c n) -> p c n", c=LC)

        def rows(a, h0, h1):
            return a.rearrange("p c (b h) -> p c b h", b=BT)[:, :, :, h0:h1]

        block = ctx.enter_context(nc.Block())

        @block.sync
        def _(sp):
            sp.dma_start(par[:, :, :], params).then_inc(par_in, 16)
            sp.dma_start(tab[:, :, :], table).then_inc(table_in, 16)
            sp.dma_start(d_sb[:, :], d_row).then_inc(d_in, 16)
            sp.dma_start(ids[:, :], ids_all).then_inc(ids_in, 16)
            sp.dma_start(row_c[:, :], row_of).then_inc(row_in, 16)
            for n in range(NW):
                sp.dma_start(x_t[:, n, :], b_rows[n * BC:(n + 1) * BC, :]).then_inc(chunk_in[n], 16)
            sp.wait_ge(zeroed, 1)
            sp.dma_start(k_pad[:, 0:P], zero[:, :]).then_inc(pad_stored, 16)

            def load_x(h, s):
                sp.dma_start(x_in[:, s, :], x_conv[h]).then_inc(x_landed[s], 16)

            def load_strip(h, s):
                row = k_pad[bass.ds(h, 1), 1:1 + L]
                src = bass.AP(tensor=row.tensor, offset=row.offset, ap=[[1, P], [1, L]])
                sp.dma_start(strip[:, s, :].bitcast(F32), src).then_inc(strip_landed[s], 16)

            for s in range(2):
                load_x(s, s)
            sp.dma_start(len_sb[:, :], length.to_broadcast((P, NB))).then_inc(len_in, 16)
            sp.dma_start(a_raw[:, :, :], a_t).then_inc(a_in, 16)
            for n in range(NW):
                sp.wait_ge(tab_hi, n + 1)
                sp.dma_start(b_tab[n * BC:(n + 1) * BC, :], w_hi[:, n, :].bitcast(F32)).then_inc(tab_hi_stored, 16)
            for s in range(2, XS):
                load_x(s, s)
            sp.dma_start(w_sb[:, :, :], w_t).then_inc(w_in, 16)
            sp.dma_start(bias_sb[:, :], bias.to_broadcast((P, L))).then_inc(bias_in, 16)

            sp.wait_ge(pad_stored, 16)
            sp.wait_ge(k_stored, 16)
            for s in range(XS):
                load_strip(s, s)

            def load_head(h, s, new_group=False):
                sp.wait_ge(xc_lo_done, h + (1 - XS))
                load_x(h, s)
                if new_group:
                    sp.wait_ge(k_stored, 16 * (h // G + 1))
                sp.wait_ge(conv_done, h + (1 - XS))
                load_strip(h, s)

            for n in range(NW):
                sp.wait_ge(tab_lo, n + 1)
                o = AD * R + n * BC
                sp.dma_start(b_tab[o:o + BC, :], w_lo[:, n, :].bitcast(F32)).then_inc(tab_lo_stored, 16)
            for h in range(XS, NU + XS):
                load_head(h, h % XS, h % G == 0)
            with sp.Fori(NU // XS + 1, NH // XS) as lap:
                for s in range(XS):
                    load_head(lap * XS + s, s)

            def load_x_tile(t, s):
                sp.dma_start(x_t[:, s, :], x_tile[t]).then_inc(xt_landed[s], 16)

            def store(t, s):
                sp.wait_ge(o_done, t + 1)
                sp.dma_start(out[bass.ds(t * P, P), :], o_sb[:, s, :]).then_inc(stored[s], 16)

            sp.wait_ge(tab_lo, NW)
            def pass_tile(t, s):
                sp.wait_ge(xlo_done, t + (1 - XT))
                load_x_tile(t, s % XT)
                if not isinstance(t, int) or t >= AHEAD:
                    store(t - AHEAD, (s - AHEAD) % OS)

            for t in range(XT):
                load_x_tile(t, t)
            for t in range(XT, 2 * OS):
                pass_tile(t, t)
            with sp.Fori(2, NT // OS) as lap:
                for s in range(OS):
                    pass_tile(lap * OS + s, s)
            for t in range(NT - AHEAD, NT):
                store(t, t % OS)
            for s in range(OS):
                sp.wait_ge(stored[s], 16 * (NT // OS))

        @block.gpsimd
        def _(pool):
            steps = [0]

            def link(ins):
                steps[0] += 1
                ins.then_inc(pool_step, 1)
                pool.wait_ge(pool_step, steps[0])

            g = nc.gpsimd
            link(g.memset(zero[:, :], 0.0))
            g.memset(row0[:, :], 0.0).then_inc(zeroed, 1)
            pool.wait_ge(zeroed, 1)
            g.memset(row0[:, 0:1], 1.0).then_inc(zeroed, 1)
            g.iota(pos, pattern=[[P, LC], [0, NB]], base=0, channel_multiplier=1).then_inc(pos_ready, 1)
            link(g.memset(eye[:, :], 0.0))
            g.affine_select(out=eye[:, :], in_=eye[:, :], compare_op=ALU.not_equal, fill=1.0,
                            base=0, pattern=[[-1, P]], channel_multiplier=1).then_inc(eye_ready, 1)
            pool.wait_ge(eye_ready, 1)
            link(g.memset(own[:, :, :], 1.0))
            link(g.affine_select(out=own[:, :, :], in_=own[:, :, :], compare_op=ALU.is_ge, fill=0.0, base=0,
                                 pattern=[[-R, BT], [0, NH]], channel_multiplier=1))
            g.affine_select(out=own[:, :, :], in_=own[:, :, :], compare_op=ALU.is_ge, fill=0.0, base=R - 1,
                            pattern=[[R, BT], [0, NH]], channel_multiplier=-1).then_inc(own_ready, 1)
            pool.wait_ge(own_ready, 1)
            ai = par[:, 1, :]
            pool.wait_ge(par_in, 16)
            pool.wait_ge(ea_ready, 1)
            link(g.tensor_tensor(sm[:, 0, :], ea[:, :], ea[:, :], ALU.mult))
            link(g.tensor_tensor(sm[:, 1, :], ai, ai, ALU.mult))
            g.tensor_tensor(sm[:, 2, :], sm[:, 0, :], sm[:, 1, :], ALU.add).then_inc(den_ready, 1)
            pool.wait_ge(den_ready, 1)

            def twice(a):
                return a.unsqueeze(1).to_broadcast((P, 2, NH))

            link(g.tensor_tensor(sm[:, 4:6, :], par[:, 2:4, :], twice(ea[:, :]), ALU.mult))
            link(g.tensor_tensor(sm[:, 6:8, :], par[:, 4:6, :], twice(ai), ALU.mult))
            link(g.tensor_tensor(sm[:, 4, :], sm[:, 4, :], sm[:, 6, :], ALU.subtract))
            g.tensor_tensor(sm[:, 5, :], sm[:, 5, :], sm[:, 7, :], ALU.add).then_inc(m_ready, 1)
            pool.wait_ge(m_ready, 1)
            pool.wait_ge(zr_ready, 1)

            def exponents_of(h0, h1):
                n = h1 - h0
                g.tensor_tensor(mag[:, h0:h1, :], zr[:, h0:h1].unsqueeze(2).to_broadcast((P, n, NA + NC)),
                                tab[:, 0, NA:NF].unsqueeze(1).to_broadcast((P, n, NA + NC)),
                                ALU.mult).then_inc(exponents, 1)

            c, k, r, q = (sm[:, n, :] for n in range(8, 12))
            link(g.tensor_scalar(c, zr[:, :], -87.3, 88.0, ALU.max, ALU.min))
            link(g.tensor_scalar(k, c, LOG2_E, ROUND, ALU.mult, ALU.add))
            link(g.tensor_scalar(k, k, -ROUND, None, ALU.add))
            link(g.tensor_scalar(q, k, -LN2_HI, None, ALU.mult))
            link(g.tensor_tensor(r, q, c, ALU.add))
            link(g.tensor_scalar(q, k, -LN2_LO, None, ALU.mult))
            link(g.tensor_tensor(r, q, r, ALU.add))
            link(g.tensor_scalar(ez_i[:, :], k, 127.0, 2.0 ** 23, ALU.add, ALU.mult))
            link(g.tensor_scalar(q, r, 1 / 5040, 1 / 720, ALU.mult, ALU.add))
            for n in range(5, -1, -1):
                link(g.tensor_tensor(q, q, r, ALU.mult))
                link(g.tensor_scalar(q, q, 1 / math.factorial(n), None, ALU.add))
            g.tensor_tensor(ez[:, :], q, ez_i[:, :].bitcast(F32), ALU.mult).then_inc(ez_ready, 1)
            pool.wait_ge(ez_ready, 1)
            pool.wait_ge(table_in, 16)
            exponents_of(0, G)
            pool.wait_ge(exponents, 1)
            exponents_of(G, NH)
            pool.wait_ge(exponents, 2)

            def split_x(h, s):
                pool.wait_ge(xc_hi_done, h + 1)
                g.tensor_tensor(xp[:, s % CS, :, 1, :], in_chunks(x_in[:, s, :]),
                                xp[:, s % CS, :, 0, :].bitcast(F32), ALU.subtract).then_inc(xc_lo_done, 1)

            split_x(0, 0)
            for n in range(NW):
                pool.wait_ge(tab_hi, n + 1)
                g.tensor_tensor(w_lo[:, n, :], x_t[:, n, :], w_hi[:, n, :].bitcast(F32),
                                ALU.subtract).then_inc(tab_lo, 1)
            def split_w(n):
                pool.wait_ge(w_hi_done, n + 1)
                g.tensor_tensor(w_lo[:, bass.ds(n, 1), :], w_sb[:, bass.ds(n, 1), :],
                                w_hi[:, bass.ds(n, 1), :].bitcast(F32), ALU.subtract).then_inc(w_split, 1)

            for h in range(1, NU):
                split_x(h, h % XS)
                if h == 1:
                    pool.wait_ge(w_in, 16)
                    for c in range(LC):
                        d = w_sb[:, c, c * P:(c + 1) * P]
                        g.tensor_tensor(d, d, eye[:, :], ALU.add).then_inc(w_eye, 1)
                    pool.wait_ge(w_eye, LC)
                if h in (NU - 6, NU - 2):
                    pool.wait_ge(tab_lo_stored, 16 * NW)
                    split_w((h - NU + 6) // 4)
                if h % XS == 2 and h // XS < NW:
                    n = h // XS
                    pool.wait_ge(a_hi_done, 1)
                    part = slice(n * AD // NW, (n + 1) * AD // NW)
                    g.tensor_tensor(a_hl[:, part, 1, :], a_raw[:, part, :], a_hl[:, part, 0, :].bitcast(F32),
                                    ALU.subtract).then_inc(a_split, 1)

            with pool.Fori(NU // XS, NH // XS) as lap:
                for s in range(XS):
                    split_x(lap * XS + s, s)
                    if s == 1:
                        split_w(lap + (2 - NU // XS))

            def gather(t, s):
                for q in range(QA, BT):
                    i = pool.value_load(ids[0:1, bass.ds(t * BT + q, 1)], min_val=0, max_val=AD - 1)
                    src = a_hl[:, bass.ds(i, 1), :, :].bitcast(F32).rearrange("p o e (c r) -> p (o e) c r", c=LC)
                    last = g.tensor_copy(ag[:, s, :, :, q, :].rearrange("p c e r -> p e c r"), src)
                last.then_inc(gathered, 1)

            def index_b(t, s):
                g.tensor_copy(b_now[:, s:s + 1], b_idx[:, bass.ds(t, 1)]).then_inc(idx_copied, 1)
                pool.wait_ge(idx_copied, t + 1)

            def gather_b(s):
                g.indirect_dma_start(out=b_hl[:, s, :].bitcast(F32), out_offset=None, in_=b_tab,
                                     in_offset=bass.IndirectOffsetOnAxis(ap=b_now[:, s:s + 1], axis=0)
                                     ).then_inc(b_landed[s], 16)

            pool.wait_ge(tab_hi_stored, 16 * NW)
            pool.wait_ge(tab_lo_stored, 16 * NW)
            pool.wait_ge(idx_ready, 1)
            pool.wait_ge(ids_ready, 1)
            pool.wait_ge(a_split, NW)
            pool.wait_ge(w_split, NW)
            for t in range(BS):
                if t >= TS:
                    pool.wait_ge(h_done, t + (1 - TS))
                gather(t, t % TS)
                pool.wait_ge(conv_done, NH - BS + t + 1)
                index_b(t, t)
                gather_b(t)
            with pool.Fori(1, NT // BS) as lap:
                for s in range(BS):
                    t = lap * BS + s
                    pool.wait_ge(y_done, t + (1 - BS))
                    index_b(t, s)
                    pool.wait_ge(h_done, t + (1 - TS))
                    gather(t, s % TS)
                    gather_b(s)

        @block.scalar
        def _(act):
            act.wait_ge(par_in, 16)
            nc.scalar.activation(ea[:, :], par[:, 0, :], ACT.Exp).then_inc(ea_ready, 1)
            for n in range(NW):
                act.wait_ge(chunk_in[n], 16)
                nc.scalar.activation(w_hi[:, n, :], x_t[:, n, :], ACT.Copy).then_inc(tab_hi, 1)

            def group_sines(k):
                act.wait_ge(reduced, k + 1)
                nc.scalar.activation(sines[:, :, :], red[:, :, :], ACT.Sin).then_inc(sines_ready, 1)

            def group_store(k):
                s = k % KS
                act.wait_ge(k_done, k + 1)
                if k >= KS:
                    act.wait_ge(k_stored, 16 * (k - 1))
                nc.scalar.activation(k_sb[:, s, :], k_ps[0:NA, s, 0:G * NC], ACT.Copy).then_inc(k_copied, 1)
                act.wait_ge(k_copied, k + 1)
                if k >= 1:
                    act.wait_ge(k_stored, 16 * k)
                act.dma_start(k_pad[k * G:(k + 1) * G, P:PAD].rearrange("h (a c) -> a h c", a=NA),
                              k_sb[:, s, :].rearrange("a (h c) -> a h c", c=NC)).then_inc(k_stored, 16)

            def split_x(h, s, lap, first):
                act.wait_ge(x_landed[s], 16 * (lap + 1))
                if not first:
                    act.wait_ge(conv_done, h + (1 - CS))
                act.activation(xp[:, s % CS, :, 0, :], in_chunks(x_in[:, s, :]),
                               ACT.Copy).then_inc(xc_hi_done, 1)

            def split_strip(h, s, lap):
                act.wait_ge(strip_landed[s], 16 * (lap + 1))
                act.activation(s_hi[:, s % CS, :], strip[:, s, :].bitcast(F32), ACT.Copy).then_inc(s_hi_done, 1)

            def split_w(n):
                act.activation(w_hi[:, bass.ds(n, 1), :], w_sb[:, bass.ds(n, 1), :], ACT.Copy).then_inc(w_hi_done, 1)

            group_sines(0)
            act.wait_ge(angle_ready, 1)
            nc.scalar.activation(cs[:, :, :], an[:, 0, :, :], ACT.Sin).then_inc(cs_ready, 1)
            split_x(0, 0, 0, True)
            split_x(1, 1, 0, True)
            for n, (h0, h1) in enumerate(((0, G), (G, NH))):
                act.wait_ge(exponents, n + 1)
                nc.scalar.activation(mag[:, h0:h1, :], mag[:, h0:h1, :], ACT.Exp).then_inc(mags, 1)
            group_store(0)
            act.wait_ge(a_in, 16)
            nc.scalar.activation(a_hl[:, :, 0, :], a_raw[:, :, :], ACT.Copy).then_inc(a_hi_done, 1)
            group_sines(1)
            for h in range(NU):
                for k, last in K_AFTER.items():
                    if h == last + XS - (k == 1):
                        group_store(k)
                if h >= 2:
                    split_x(h, h % XS, h // XS, h < CS)
                split_strip(h, h % XS, h // XS)
                for k, at in STEPS_AT.items():
                    if h == at[-1] - 2:
                        group_sines(k)
                if h in (NU - 7, NU - 3):
                    act.wait_ge(w_eye, LC)
                    act.wait_ge(tab_hi_stored, 16 * NW)
                    split_w((h - NU + 7) // 4)
            with act.Fori(NU // XS, NH // XS) as lap:
                split_w(lap + (2 - NU // XS))
                for s in range(XS):
                    split_x(lap * XS + s, s, lap, False)
                    split_strip(lap * XS + s, s, lap)

            def gather(t, s):
                for q in range(QA):
                    i = act.value_load(ids[0:1, bass.ds(t * BT + q, 1)], min_val=0, max_val=AD - 1)
                    src = a_hl[:, bass.ds(i, 1), :, :].bitcast(F32).rearrange("p o e (c r) -> p (o e) c r", c=LC)
                    for e in range(2):
                        last = act.activation(ag[:, s, :, e, q, :], src[:, e, :, :], ACT.Copy)
                last.then_inc(act_gathered, 1)

            def x1_hi(t, s, first):
                act.wait_ge(x1_done, t + 1)
                if not first:
                    act.wait_ge(base_done, t + (1 - HS))
                act.activation(xp[:, s % HS, :, 0, :], in_chunks(x_t[:, s % XT, :]), ACT.Copy).then_inc(xhi_done, 1)

            def h_down(t, b):
                act.wait_ge(h_done, t + 1)
                act.activation(h_b[:, b, :], h_ps[BR:P, b, 0:2 * P], ACT.Copy).then_inc(hb_done, 1)

            def h_rounded(t, b, first):
                act.wait_ge(hm_done, t + 1)
                if not first:
                    act.wait_ge(y_done, t + (1 - TS))
                for o in (0, BR):
                    act.activation(h_hi[o:o + BR, b, :], h_m[:, b, :], ACT.Copy).then_inc(hhi_done, 1)

            def step(i, s):
                known, b = isinstance(i, int), (s + 1) % TS
                if not known or i + 3 < NT:
                    x1_hi(i + 3, s + 3, known and i + 3 < HS)
                h_down(i + 1, b)
                if not known or i + 3 < NT:
                    gather(i + 3, b)
                h_rounded(i + 1, b, known and i + 1 < TS)

            act.wait_ge(ids_ready, 1)
            act.wait_ge(a_split, NW)
            act.wait_ge(x1_early, 1)
            act.activation(rows(xp[:, 0, :, 0, :], 0, EARLY), rows(in_chunks(x_t[:, 0, :]), 0, EARLY),
                           ACT.Copy).then_inc(xhi_early, 1)
            gather(0, 0)
            act.wait_ge(x1_done, 1)
            act.activation(rows(xp[:, 0, :, 0, :], EARLY, NH), rows(in_chunks(x_t[:, 0, :]), EARLY, NH),
                           ACT.Copy).then_inc(xhi_done, 1)
            gather(1, 1)
            h_down(0, 0)
            x1_hi(1, 1, True)
            h_rounded(0, 0, True)
            x1_hi(2, 2, True)
            gather(2, 0)
            for i in range(0, 2):
                step(i, i)
            with act.Fori(0, NT // OS - 2) as lap:
                for s in range(2, OS + 2):
                    step(lap * OS + s, s)
            for i in range(NT - OS - 2, NT - 1):
                step(i, i % OS)

        @block.vector
        def _(dve):
            steps = [0]

            def link(ins):
                steps[0] += 1
                ins.then_inc(dve_step, 1)
                dve.wait_ge(dve_step, steps[0])

            V = nc.vector
            def exp(dst, x):
                c, k, r, q = (ex[:, n, :] for n in range(4))
                link(V.tensor_scalar(c, x, -87.3, 88.0, ALU.max, ALU.min))
                link(V.tensor_scalar(k, c, LOG2_E, ROUND, ALU.mult, ALU.add))
                link(V.tensor_scalar(k, k, -ROUND, None, ALU.add))
                link(V.scalar_tensor_tensor(r, k, -LN2_HI, c, ALU.mult, ALU.add))
                link(V.scalar_tensor_tensor(r, k, -LN2_LO, r, ALU.mult, ALU.add))
                link(V.tensor_scalar(ex_i[:, :], k, 127.0, 2.0 ** 23, ALU.add, ALU.mult))
                link(V.tensor_scalar(q, r, 1 / 5040, None, ALU.mult))
                for n in range(6, 0, -1):
                    link(V.scalar_tensor_tensor(q, q, 1 / math.factorial(n), r, ALU.add, ALU.mult))
                return V.scalar_tensor_tensor(dst, q, 1.0, ex_i[:, :].bitcast(F32), ALU.add, ALU.mult)

            dve.wait_ge(par_in, 16)
            link(exp(dt[:, :], par[:, 6, :]))
            dve.wait_ge(ea_ready, 1)
            V.scalar_tensor_tensor(zr[:, :], ea[:, :], -1.0, dt[:, :], ALU.mult, ALU.mult).then_inc(zr_ready, 1)
            link(V.tensor_tensor(zi[:, :], par[:, 1, :], dt[:, :], ALU.mult))

            def small_angles():
                for n, turns in ((0, 0.25), (1, 0.0)):
                    V.tensor_scalar(an[:, 1, n, :], zi[:, :], 1 / (2 * math.pi), turns, ALU.mult,
                                    ALU.add).then_inc(dve_step, 1)
                steps[0] += 2
                dve.wait_ge(dve_step, steps[0])
                turns, angle = an[:, 1, :, :], an[:, 0, :, :]
                link(V.tensor_scalar(turns, turns, ROUND, -ROUND, ALU.add, ALU.add))
                link(V.scalar_tensor_tensor(angle, turns, -TWO_PI_HI, zi[:, :].unsqueeze(1).to_broadcast((P, 2, NH)),
                                            ALU.mult, ALU.add))
                link(V.scalar_tensor_tensor(angle, turns, -TWO_PI_LO, angle, ALU.mult, ALU.add))
                link(V.tensor_scalar(an[:, 0, 0, :], an[:, 0, 0, :], math.pi / 2, None, ALU.add))
                V.tensor_scalar(angle, angle, -PI, PI, ALU.max, ALU.min).then_inc(angle_ready, 1)

            def scale_m():
                dve.wait_ge(m_ready, 1)
                dve.wait_ge(den_ready, 2)
                link(V.scalar_tensor_tensor(sm[:, 4:6, :], sm[:, 4:6, :], -2.0,
                                            sm[:, 3, :].unsqueeze(1).to_broadcast((P, 2, NH)), ALU.mult, ALU.mult))

            def adapter_ids():
                dve.wait_ge(ids_in, 16)
                dve.wait_ge(row_in, 16)
                link(V.tensor_copy(id_f[:, 1, :], ids[:, :]))
                link(V.tensor_scalar(id_f[:, 0, :], id_f[:, 1, :], 0.0, float(AD), ALU.is_lt, ALU.mult))
                link(V.tensor_tensor(id_f[:, 1, :], id_f[:, 1, :], id_f[:, 0, :], ALU.add))
                link(V.tensor_scalar(id_f[:, 0, :], id_f[:, 1, :], 0.0, float(AD - 1), ALU.max, ALU.min))
                V.tensor_copy(ids[:, :], id_f[:, 0, :]).then_inc(ids_ready, 1)
                dve.wait_ge(ids_ready, 1)
                V.tensor_scalar(b_idx[:, :], ids[:, NB:NB + NT], float(R), row_c[:, :], ALU.mult,
                                ALU.add).then_inc(idx_ready, 1)

            dve.wait_ge(den_ready, 1)
            V.reciprocal(sm[:, 3, :], sm[:, 2, :]).then_inc(den_ready, 1)

            cr, ci = sm[:, 14, :], sm[:, 15, :]

            def ct():
                dve.wait_ge(ez_ready, 1)
                dve.wait_ge(cs_ready, 1)
                link(V.tensor_tensor(cs[:, :, :], cs[:, :, :], ez[:, :].unsqueeze(1).to_broadcast((P, 2, NH)), ALU.mult))
                link(V.tensor_scalar(cs[:, 0, :], cs[:, 0, :], -1.0, None, ALU.add))
                link(V.tensor_tensor(cs_m[:, 0:2, :], cs[:, :, :], sm[:, 4, :].unsqueeze(1).to_broadcast((P, 2, NH)),
                                     ALU.mult))
                link(V.tensor_tensor(cs_m[:, 2:4, :], cs[:, :, :], sm[:, 5, :].unsqueeze(1).to_broadcast((P, 2, NH)),
                                     ALU.mult))
                link(V.tensor_tensor(cr, cs_m[:, 0, :], cs_m[:, 3, :], ALU.subtract))
                link(V.tensor_tensor(ci, cs_m[:, 1, :], cs_m[:, 2, :], ALU.add))

            l_col = tab[:, 0, :].unsqueeze(1).to_broadcast((P, G, NF))
            turn_col = tab[:, 1, :].unsqueeze(1).to_broadcast((P, G, NF))
            phase_col = tab[:, 2, :].unsqueeze(1).to_broadcast((P, G, NF))

            def group(k):
                hs, s = slice(k * G, (k + 1) * G), k % KS
                wide = lambda a, n: a[:, hs].unsqueeze(2).to_broadcast((P, G, n))

                def angles():
                    link(V.tensor_tensor(ang[:, :, :], wide(zi, NF), l_col, ALU.mult))

                def whole_turns():
                    link(V.scalar_tensor_tensor(trn[:, :, :], ang[:, :, :], 1 / (2 * math.pi), turn_col,
                                                ALU.mult, ALU.add))
                    link(V.tensor_scalar(trn[:, :, :], trn[:, :, :], ROUND, -ROUND, ALU.add, ALU.add))

                def reduce_hi():
                    if k:
                        dve.wait_ge(sines_ready, k)
                    link(V.scalar_tensor_tensor(red[:, :, :], trn[:, :, :], -TWO_PI_HI, ang[:, :, :],
                                                ALU.mult, ALU.add))

                def reduce_lo():
                    link(V.scalar_tensor_tensor(red[:, :, :], trn[:, :, :], -TWO_PI_LO, red[:, :, :],
                                                ALU.mult, ALU.add))

                def bound():
                    link(V.tensor_tensor(red[:, :, :], red[:, :, :], phase_col, ALU.add))
                    V.tensor_scalar(red[:, :, :], red[:, :, :], -PI, PI, ALU.max, ALU.min).then_inc(reduced, 1)

                def multiply():
                    dve.wait_ge(sines_ready, k + 1)
                    if k >= KS:
                        dve.wait_ge(k_done, k + 1 - KS)
                    link(V.tensor_tensor(gg[:, s, :, :], sines[:, :, 0:NA], wide(cr, NA), ALU.mult))
                    link(V.tensor_tensor(g2[:, :, :], sines[:, :, NA:2 * NA], wide(ci, NA), ALU.mult))
                    link(V.tensor_tensor(gg[:, s, :, :], gg[:, s, :, :], g2[:, :, :], ALU.add))

                def scale():
                    dve.wait_ge(mags, 1 if k == 0 else 2)
                    V.tensor_tensor(gg[:, s, :, :], gg[:, s, :, :], mag[:, hs, 0:NA], ALU.mult).then_inc(factors, 1)
                    V.tensor_tensor(ee[:, s, :, :], sines[:, :, 2 * NA:NF], mag[:, hs, NA:NA + NC],
                                    ALU.mult).then_inc(factors, 1)

                return [angles, whole_turns, reduce_hi, reduce_lo, bound, multiply, scale]

            dve.wait_ge(table_in, 16)
            for k in range(2):
                todo = group(k)
                if k == 0:
                    todo[5:5] = [small_angles, adapter_ids, scale_m, ct]
                for do in todo:
                    do()
                if k == 0:
                    dve.wait_ge(pos_ready, 1)
                    dve.wait_ge(len_in, 16)
                    link(V.tensor_tensor(mask[:, :, :], pos,
                                         len_sb[:, :].unsqueeze(1).to_broadcast((P, LC, NB)), ALU.is_lt))

            m2 = mask[:, :, :].rearrange("p c b -> p (c b)")

            def split(h, s):
                dve.wait_ge(s_hi_done, h + 1)
                V.tensor_tensor(strip[:, s, :], strip[:, s, :].bitcast(F32), s_hi[:, s % CS, :].bitcast(F32),
                                ALU.subtract).then_inc(s_lo_done, 1)

            def head(h, s):
                dve.wait_ge(conv_done, h + 1)
                V.tensor_tensor(z_all[:, :, :, bass.ds(h, 1)].rearrange("p c b o -> p (c b o)"),
                                z_ps[:, s % ZS, :], m2, ALU.mult).then_inc(z_masked, 1)

            beside = {h: do for k, at in STEPS_AT.items() for h, do in zip(at, group(k))}
            for h in range(NU):
                split(h, h % XS)
                if h >= 2:
                    head(h - 2, (h - 2) % XS)
                if h in beside:
                    beside[h]()
            with dve.Fori(NU // XS, NH // XS) as lap:
                for s in range(XS):
                    split(lap * XS + s, s)
                    head(lap * XS + (s - 2), (s - 2) % XS)
            def x1_of(t, s, lap):
                dve.wait_ge(xt_landed[s % XT], 16 * (lap + 1))
                xt = in_chunks(x_t[:, s % XT, :])
                V.tensor_tensor(xt, xt, z_all[:, :, bass.ds(t * BT, BT), :].rearrange("p c b h -> p c (b h)"),
                                ALU.add).then_inc(x1_done, 1)

            def x1_remainder(t, s):
                dve.wait_ge(xhi_done, t + 1)
                V.tensor_tensor(xp[:, s % HS, :, 1, :], in_chunks(x_t[:, s % XT, :]),
                                xp[:, s % HS, :, 0, :].bitcast(F32), ALU.subtract).then_inc(xlo_done, 1)

            def h_masked(t, b):
                dve.wait_ge(hb_done, t + 1)
                V.tensor_tensor(h_s[:, b, :], h_ps[0:BR, b, 0:2 * P], h_b[:, b, :], ALU.add).then_inc(hs_done, 1)
                dve.wait_ge(hs_done, t + 1)
                V.tensor_tensor(h_s[:, b, 0:P], h_s[:, b, 0:P], h_s[:, b, P:2 * P], ALU.add).then_inc(h2_done, 1)
                dve.wait_ge(h2_done, t + 1)
                V.tensor_tensor(h_m[:, b, :], h_s[:, b, 0:P], own[:, :, :].rearrange("p b h -> p (b h)"),
                                ALU.mult).then_inc(hm_done, 1)

            def h_remainder(t, b):
                dve.wait_ge(hhi_done, 2 * t + 2)
                V.tensor_tensor(h_lo[:, b, :], h_m[:, b, :], h_hi[0:BR, b, :].bitcast(F32),
                                ALU.subtract).then_inc(hlo_done, 1)

            def step(i, s, lap):
                known = isinstance(i, int)

                def there(t):
                    return not known or 0 <= t < NT

                if there(i - 1):
                    dve.wait_ge(y_done, i)
                    if not known or i - 1 >= OS:
                        dve.wait_ge(stored[(s - 1) % OS], 16 * (lap + (s - 1) // OS))
                    V.tensor_tensor(o_sb[:, (s - 1) % OS, :], y_ps[:, (s - 1) % TS, :], bias_sb[:, :],
                                    ALU.add).then_inc(o_done, 1)
                if there(i + 4):
                    x1_of(i + 4, s + 4, lap + (s + 4) // XT)
                if there(i + 1):
                    h_masked(i + 1, (s + 1) % TS)
                if there(i + 3):
                    x1_remainder(i + 3, s + 3)
                if there(i + 1):
                    h_remainder(i + 1, (s + 1) % TS)

            def part_of_x1(h0, h1, done):
                V.tensor_tensor(rows(in_chunks(x_t[:, 0, :]), h0, h1), rows(in_chunks(x_t[:, 0, :]), h0, h1),
                                z_all[:, :, 0:BT, h0:h1], ALU.add).then_inc(done, 1)

            def part_of_remainder(h0, h1, done):
                V.tensor_tensor(rows(xp[:, 0, :, 1, :], h0, h1), rows(in_chunks(x_t[:, 0, :]), h0, h1),
                                rows(xp[:, 0, :, 0, :].bitcast(F32), h0, h1), ALU.subtract).then_inc(done, 1)

            def last_head(b0, b1):
                h = NH - 1
                V.tensor_tensor(z_all[:, :, b0:b1, h:NH].rearrange("p c b o -> p c (b o)"),
                                in_chunks(z_ps[:, h % ZS, :])[:, :, b0:b1], mask[:, :, b0:b1],
                                ALU.mult).then_inc(z_masked, 1)

            dve.wait_ge(xt_landed[0], 16)
            dve.wait_ge(z_masked, EARLY)
            part_of_x1(0, EARLY, x1_early)
            head(NH - 2, (NH - 2) % XS)
            dve.wait_ge(xhi_early, 1)
            part_of_remainder(0, EARLY, xlo_early)
            dve.wait_ge(conv_done, NH)
            last_head(0, BT)
            dve.wait_ge(z_masked, NH)
            part_of_x1(EARLY, NH, x1_done)
            dve.wait_ge(xhi_done, 1)
            part_of_remainder(EARLY, NH, xlo_done)
            last_head(BT, NB)
            dve.wait_ge(own_ready, 1)
            dve.wait_ge(bias_in, 16)
            dve.wait_ge(z_masked, NH + 1)
            x1_of(1, 1, 0)
            h_masked(0, 0)
            x1_remainder(1, 1)
            x1_of(2, 2, 0)
            h_remainder(0, 0)
            x1_remainder(2, 2)
            x1_of(3, 3, 0)
            for i in range(OS + 1):
                step(i, i % OS, i // OS)
            with dve.Fori(1, NT // OS - 2) as lap:
                for s in range(1, OS + 1):
                    step(lap * OS + s, s, lap)
            for i in range(NT - 2 * OS + 1, NT + 1):
                step(i, i % OS, i // OS)

        @block.tensor
        def _(pe):
            pe.wait_ge(d_in, 16)
            pe.wait_ge(zeroed, 2)

            def keep_warm(n):
                for _ in range(n):
                    nc.tensor.matmul(y_ps[:, 0, 0:P], eye[:, :], eye[:, :], start=True, stop=True)

            def group(k):
                s = k % KS
                pe.wait_ge(factors, 2 * (k + 1))
                if k >= KS:
                    pe.wait_ge(k_copied, k + 1 - KS)
                for i in range(G):
                    nc.tensor.matmul(k_ps[0:NA, s, i * NC:(i + 1) * NC], gg[:, s, i, :], ee[:, s, i, :],
                                     start=(i == 0), stop=False)
                nc.tensor.matmul(k_ps[0:NA, s, 0:G * NC:NC], row0[:, :], d_sb[:, k * G:(k + 1) * G],
                                 start=False, stop=True).then_inc(k_done, 1)

            def head(h, s, first):
                pe.wait_ge(xc_lo_done, h + 1)
                pe.wait_ge(s_lo_done, h + 1)
                if not first:
                    pe.wait_ge(z_masked, h + (1 - ZS))
                terms = [(m, t, e) for m in range(LC) for t, e in ((s_hi, 0), (s_hi, 1), (strip, 0))]
                for n, (m, t, e) in enumerate(terms):
                    last = nc.tensor.matmul(z_ps[:, s % ZS, m * P:L], t[:, s % CS, m * P:(m + 1) * P],
                                            xp[:, s % CS, 0:LC - m, e, :], start=(n == 0), stop=(n == len(terms) - 1))
                last.then_inc(conv_done, 1)

            group(0)
            pe.wait_ge(eye_ready, 1)
            pe.wait_ge(reduced, 2)
            keep_warm(5)
            for h in range(NU):
                head(h, h % XS, h < ZS)
                for k, last in K_AFTER.items():
                    if h == last:
                        group(k)
            with pe.Fori(NU // XS, NH // XS) as lap:
                for s in range(XS):
                    head(lap * XS + s, s, False)

            def tile_h(t, s, first):
                pe.wait_ge(gathered, t + 1)
                pe.wait_ge(act_gathered, t + 1)
                pe.wait_ge(xlo_done, t + 1)
                if not first:
                    pe.wait_ge(hs_done, t + (1 - TS))
                for c in range(LC):
                    last = nc.tensor.matmul(h_ps[:, s % TS, 0:2 * P],
                                            ag[:, s % TS, c, :, :, :].rearrange("p e b r -> p (e b r)"),
                                            xp[:, s % HS, c, :, :].rearrange("p e n -> p (e n)"),
                                            start=(c == 0), stop=(c == LC - 1))
                last.then_inc(h_done, 1)

            def tile_base(t, s, first):
                if not first:
                    pe.wait_ge(o_done, t + (1 - TS))
                terms = [(c, e, w) for c in range(LC) for e, w in ((0, w_hi), (0, w_lo), (1, w_hi))]
                for n, (c, e, w) in enumerate(terms):
                    last = nc.tensor.matmul(y_ps[:, s % TS, :], xp[:, s % HS, c, e, :], w[:, c, :],
                                            start=(n == 0), stop=False)
                last.then_inc(base_done, 1)

            def tile_b(t, s, lap):
                b = s % TS
                pe.wait_ge(b_landed[s % BS], 16 * (lap + 1))
                pe.wait_ge(hlo_done, t + 1)
                nc.tensor.matmul(y_ps[:, b, :], h_hi[:, b, :], b_hl[:, s % BS, :], start=False, stop=False)
                nc.tensor.matmul(y_ps[:, b, :], h_lo[:, b, :], b_hl[0:BR, s % BS, :],
                                 start=False, stop=True).then_inc(y_done, 1)

            pe.wait_ge(z_masked, EARLY)
            pe.wait_ge(w_split, NW)
            pe.wait_ge(xlo_early, 1)
            tile_h(0, 0, True)
            for t in range(TS):
                tile_base(t, t, True)
                tile_h(t + 1, t + 1, t + 1 < TS)
                tile_b(t, t, 0)
            for t in range(TS, OS):
                tile_h(t + 1, t + 1, False)
                tile_base(t, t, False)
                tile_b(t, t, 0)
            with pe.Fori(1, NT // OS - 1) as lap:
                for s in range(OS):
                    t = lap * OS + s
                    tile_h(t + 1, s + 1, False)
                    tile_base(t, s, False)
                    tile_b(t, s, lap)
            for t in range(NT - OS, NT):
                if t + 1 < NT:
                    tile_h(t + 1, t + 1, False)
                tile_base(t, t, False)
                tile_b(t, t, NT // OS - 1)


def kernel(**inputs):
    import numpy as np
    import concourse.bacc as bacc
    from concourse.bass_utils import run_bass_kernel_spmd

    g = {k: np.asarray(v) for k, v in inputs.items()}

    def both(a):
        return np.concatenate([a.T, a.T], axis=0)

    c = g["L0_cond_C"]
    params = np.stack([both(g["L0_cond_log_A_real"]), both(g["L0_cond_A_imag"]), both(c[..., 0]), both(c[..., 1]),
                       both(c[..., 1]), both(c[..., 0]),
                       np.broadcast_to(g["L0_cond_log_dt"][None, :], (P, NH))], axis=1)
    table = np.zeros((P, 3, NF), np.float32)
    table[:, 0] = np.concatenate([NC * np.arange(NA), NC * np.arange(NA), np.arange(NC)])
    for half, phases in enumerate(((0.25, 0.5, 0.25), (0.0, 0.25, 0.5))):
        turns = np.repeat(phases, (NA, NA, NC))
        table[half * NS:(half + 1) * NS, 1] = turns
        table[half * NS:(half + 1) * NS, 2] = 2 * math.pi * turns
    ids = g["itok_B_6_15"]
    arrays = {
        "x_conv": g["x"].transpose(1, 2, 0).reshape(NH, LC, P, NB).transpose(0, 2, 1, 3)[:, ::-1].reshape(NH, P, L),
        "x_tile": g["x"].reshape(NT, P, LC, P).transpose(0, 3, 2, 1).reshape(NT, P, L),
        "params": params,
        "table": table,
        "d_row": g["L0_cond_D"].reshape(1, NH),
        "length": g["itok_B_78_3631"].reshape(1, NB),
        "ids_all": np.concatenate([np.broadcast_to(ids, (P, NB)), np.broadcast_to(
            ids.reshape(1, NT, BT, 1), (2, NT, BT, R)).transpose(0, 2, 3, 1).reshape(P, NT)], axis=1),
        "w_t": g["L1_cond_base_weight"].T.reshape(LC, P, L).transpose(1, 0, 2),
        "bias": g["L1_cond_base_bias"].reshape(1, L),
        "a_t": g["L1_cond_lora_A_w"].reshape(AD, R, LC, P).transpose(3, 0, 2, 1).reshape(P, AD, LC * R),
        "b_rows": g["L1_cond_lora_B_w"].transpose(0, 2, 1).reshape(AD * R, L),
        "row_of": (AD * R * (np.arange(P) // BR) + np.arange(P) % R).astype(np.float32).reshape(P, 1),
    }
    arrays = {k: np.ascontiguousarray(v) for k, v in arrays.items()}
    nc = bacc.Bacc("TRN2", target_bir_lowering=False, num_devices=1)
    args = [nc.dram_tensor(k, a.shape, mybir.dt.from_np(a.dtype), kind="ExternalInput").ap()
            for k, a in arrays.items()]
    args.append(nc.dram_tensor("out", (NB * NH, L), F32, kind="ExternalOutput").ap())
    build(nc, *args)
    r = run_bass_kernel_spmd(nc, [arrays], core_ids=[0])
    return r.results[0]["out"].reshape(NB, NH, L)
```
